# Optimizing a Trainium2 kernel written in Bass

```python
import numpy as np
import jax
import jax.numpy as jnp

def _softmax(x, axis=-1):
    return jax.nn.softmax(x, axis=axis)

def _gelu(x):
    return jax.nn.gelu(x, approximate=True)

def _silu(x):
    return jax.nn.silu(x)

def _sigmoid(x):
    return jax.nn.sigmoid(x)

def _layernorm(x, axis=-1, eps=1e-05):
    m = jnp.mean(x, axis=axis, keepdims=True)
    v = jnp.var(x, axis=axis, keepdims=True)
    return (x - m) / jnp.sqrt(v + eps)

def _scatter_add(tgt, idx, src, axis=0):
    return tgt.at[idx].add(src)

def _segment_sum(src, seg, n):
    return jax.ops.segment_sum(src, seg, n)
kernel_name = 'mk_xattn_seq_d1_seqx_r4_c0a098'

def setup_inputs(seed: int=0):
    np.random.seed(seed)
    _w = jnp.asarray

    def _rec_inputs():
        import jax
        import jax.numpy as jnp
        _rk = jax.random.key(seed)
        x = 7.22e-05 + 1 * jax.random.normal(jax.random.fold_in(_rk, 1), (2, 1024, 256), jnp.float32)
        _lenS = 1024 - jax.random.randint(jax.random.fold_in(_rk, 7), (2,), 0, max(1, 1024 // 4) + 1, jnp.int32)
        _lenS2 = 154 - jax.random.randint(jax.random.fold_in(_rk, 8), (2,), 0, max(1, 154 // 4) + 1, jnp.int32)
        _ctx_768P = jax.random.normal(jax.random.fold_in(_rk, 11), (2, 16, 192), jnp.float32)
        _ctx_768c = jax.random.dirichlet(jax.random.fold_in(_rk, 511), 0.3 * jnp.ones((16,), jnp.float32), (2, 154))
        _ctx_768t = jnp.einsum('bsk,bkd->bsd', _ctx_768c, _ctx_768P)
        _ctx_768t = _ctx_768t * jax.lax.rsqrt(jnp.mean(jnp.square(_ctx_768t)) + 1e-12) * 0.953939
        ctx_768 = -0.00055796 + 0.999787 * (_ctx_768t + 0.3 * jax.random.normal(jax.random.fold_in(_rk, 611), (2, 154, 192), jnp.float32))
        return (x, ctx_768)
    x, ctx_768 = _rec_inputs()

    def _L0_xattn_setup():
        import jax, jax.numpy as jnp
        import numpy as np
        D_MODEL = 256
        D_COND = 192
        N_HEADS = 16
        D_HEAD = 64
        D_ATTN = N_HEADS * D_HEAD
        D_FF = 4 * D_MODEL

        def _layernorm(x, g, b, eps=1e-05):
            mu = jnp.mean(x, axis=-1, keepdims=True)
            var = jnp.var(x, axis=-1, keepdims=True)
            return (x - mu) * jax.lax.rsqrt(var + eps) * g + b

        def _attention(xq, xkv, wq, wk, wv, wo, bo):
            B, S, _ = xq.shape
            T = xkv.shape[1]
            q = (xq @ wq).reshape(B, S, N_HEADS, D_HEAD)
            k = (xkv @ wk).reshape(B, T, N_HEADS, D_HEAD)
            v = (xkv @ wv).reshape(B, T, N_HEADS, D_HEAD)
            scale = D_HEAD ** (-0.5)
            attn = jnp.einsum('bihd,bjhd->bhij', q, k) * scale
            attn = jax.nn.softmax(attn, axis=-1)
            out = jnp.einsum('bhij,bjhd->bihd', attn, v).reshape(B, S, D_ATTN)
            return out @ wo + bo
        key = jax.random.key(seed)
        ks = jax.random.split(key, 16)
        B, S, T = (8, 256, 64)
        n = jax.random.normal
        inp = {'x': n(ks[0], (B, S, D_MODEL), jnp.float32), 'cond_emb': n(ks[1], (B, T, D_COND), jnp.float32), 'ln1_g': jnp.ones((D_MODEL,), jnp.float32), 'ln1_b': jnp.zeros((D_MODEL,), jnp.float32), 'ln2_g': jnp.ones((D_MODEL,), jnp.float32), 'ln2_b': jnp.zeros((D_MODEL,), jnp.float32), 'ln3_g': jnp.ones((D_MODEL,), jnp.float32), 'ln3_b': jnp.zeros((D_MODEL,), jnp.float32), 'sa_wq': n(ks[2], (D_MODEL, D_ATTN), jnp.float32) * D_MODEL ** (-0.5), 'sa_wk': n(ks[3], (D_MODEL, D_ATTN), jnp.float32) * D_MODEL ** (-0.5), 'sa_wv': n(ks[4], (D_MODEL, D_ATTN), jnp.float32) * D_MODEL ** (-0.5), 'sa_wo': n(ks[5], (D_ATTN, D_MODEL), jnp.float32) * D_ATTN ** (-0.5), 'sa_bo': jnp.zeros((D_MODEL,), jnp.float32), 'ca_wq': n(ks[6], (D_MODEL, D_ATTN), jnp.float32) * D_MODEL ** (-0.5), 'ca_wk': n(ks[7], (D_COND, D_ATTN), jnp.float32) * D_COND ** (-0.5), 'ca_wv': n(ks[8], (D_COND, D_ATTN), jnp.float32) * D_COND ** (-0.5), 'ca_wo': n(ks[9], (D_ATTN, D_MODEL), jnp.float32) * D_ATTN ** (-0.5), 'ca_bo': jnp.zeros((D_MODEL,), jnp.float32), 'ff_w1': n(ks[10], (D_MODEL, 2 * D_FF), jnp.float32) * D_MODEL ** (-0.5), 'ff_b1': jnp.zeros((2 * D_FF,), jnp.float32), 'ff_w2': n(ks[11], (D_FF, D_MODEL), jnp.float32) * D_FF ** (-0.5), 'ff_b2': jnp.zeros((D_MODEL,), jnp.float32)}
        return inp
    _L0_xattn_all = _L0_xattn_setup()
    _L0_xattn_in = {k: v for k, v in _L0_xattn_all.items() if k in ('ln1_g', 'ln1_b', 'ln2_g', 'ln2_b', 'ln3_g', 'ln3_b', 'sa_wq', 'sa_wk', 'sa_wv', 'sa_wo', 'sa_bo', 'ca_wq', 'ca_wk', 'ca_wv', 'ca_wo', 'ca_bo', 'ff_w1', 'ff_b1', 'ff_w2', 'ff_b2')}
    del _L0_xattn_all
    return {'x': x, 'ctx_768': ctx_768, 'L0_xattn_ln1_g': _L0_xattn_in['ln1_g'], 'L0_xattn_ln1_b': _L0_xattn_in['ln1_b'], 'L0_xattn_ln2_g': _L0_xattn_in['ln2_g'], 'L0_xattn_ln2_b': _L0_xattn_in['ln2_b'], 'L0_xattn_ln3_g': _L0_xattn_in['ln3_g'], 'L0_xattn_ln3_b': _L0_xattn_in['ln3_b'], 'L0_xattn_sa_wq': _L0_xattn_in['sa_wq'], 'L0_xattn_sa_wk': _L0_xattn_in['sa_wk'], 'L0_xattn_sa_wv': _L0_xattn_in['sa_wv'], 'L0_xattn_sa_wo': _L0_xattn_in['sa_wo'], 'L0_xattn_sa_bo': _L0_xattn_in['sa_bo'], 'L0_xattn_ca_wq': _L0_xattn_in['ca_wq'], 'L0_xattn_ca_wk': _L0_xattn_in['ca_wk'], 'L0_xattn_ca_wv': _L0_xattn_in['ca_wv'], 'L0_xattn_ca_wo': _L0_xattn_in['ca_wo'], 'L0_xattn_ca_bo': _L0_xattn_in['ca_bo'], 'L0_xattn_ff_w1': _L0_xattn_in['ff_w1'], 'L0_xattn_ff_b1': _L0_xattn_in['ff_b1'], 'L0_xattn_ff_w2': _L0_xattn_in['ff_w2'], 'L0_xattn_ff_b2': _L0_xattn_in['ff_b2']}

def reference(x, ctx_768, L0_xattn_ln1_g, L0_xattn_ln1_b, L0_xattn_ln2_g, L0_xattn_ln2_b, L0_xattn_ln3_g, L0_xattn_ln3_b, L0_xattn_sa_wq, L0_xattn_sa_wk, L0_xattn_sa_wv, L0_xattn_sa_wo, L0_xattn_sa_bo, L0_xattn_ca_wq, L0_xattn_ca_wk, L0_xattn_ca_wv, L0_xattn_ca_wo, L0_xattn_ca_bo, L0_xattn_ff_w1, L0_xattn_ff_b1, L0_xattn_ff_w2, L0_xattn_ff_b2):
    import jax
    import jax.numpy as jnp

    def _L0_xattn_ref(x, cond_emb, ln1_g, ln1_b, ln2_g, ln2_b, ln3_g, ln3_b, sa_wq, sa_wk, sa_wv, sa_wo, sa_bo, ca_wq, ca_wk, ca_wv, ca_wo, ca_bo, ff_w1, ff_b1, ff_w2, ff_b2):
        import jax, jax.numpy as jnp
        import numpy as np
        D_MODEL = 256
        D_COND = 192
        N_HEADS = 16
        D_HEAD = 64
        D_ATTN = N_HEADS * D_HEAD
        D_FF = 4 * D_MODEL

        def _layernorm(x, g, b, eps=1e-05):
            mu = jnp.mean(x, axis=-1, keepdims=True)
            var = jnp.var(x, axis=-1, keepdims=True)
            return (x - mu) * jax.lax.rsqrt(var + eps) * g + b

        def _attention(xq, xkv, wq, wk, wv, wo, bo):
            B, S, _ = xq.shape
            T = xkv.shape[1]
            q = (xq @ wq).reshape(B, S, N_HEADS, D_HEAD)
            k = (xkv @ wk).reshape(B, T, N_HEADS, D_HEAD)
            v = (xkv @ wv).reshape(B, T, N_HEADS, D_HEAD)
            scale = D_HEAD ** (-0.5)
            attn = jnp.einsum('bihd,bjhd->bhij', q, k) * scale
            attn = jax.nn.softmax(attn, axis=-1)
            out = jnp.einsum('bhij,bjhd->bihd', attn, v).reshape(B, S, D_ATTN)
            return out @ wo + bo
        h = _layernorm(x, ln1_g, ln1_b)
        x = _attention(h, h, sa_wq, sa_wk, sa_wv, sa_wo, sa_bo) + x
        h = _layernorm(x, ln2_g, ln2_b)
        x = _attention(h, cond_emb, ca_wq, ca_wk, ca_wv, ca_wo, ca_bo) + x
        h = _layernorm(x, ln3_g, ln3_b)
        p = h @ ff_w1 + ff_b1
        a, gate = (p[..., :D_FF], p[..., D_FF:])
        h = a * jax.nn.gelu(gate, approximate=False) @ ff_w2 + ff_b2
        return h + x
    x = _L0_xattn_ref(x, ctx_768, L0_xattn_ln1_g, L0_xattn_ln1_b, L0_xattn_ln2_g, L0_xattn_ln2_b, L0_xattn_ln3_g, L0_xattn_ln3_b, L0_xattn_sa_wq, L0_xattn_sa_wk, L0_xattn_sa_wv, L0_xattn_sa_wo, L0_xattn_sa_bo, L0_xattn_ca_wq, L0_xattn_ca_wk, L0_xattn_ca_wv, L0_xattn_ca_wo, L0_xattn_ca_bo, L0_xattn_ff_w1, L0_xattn_ff_b1, L0_xattn_ff_w2, L0_xattn_ff_b2)
    return x

_drawn_inputs = setup_inputs


def setup_inputs(seed=0):
    import zlib

    import numpy as np

    out = dict(_drawn_inputs(seed))
    spreads = {'L0_xattn_ln1_g': (1.0, 0.2),
     'L0_xattn_ln1_b': (0.0, 0.1),
     'L0_xattn_ln2_g': (1.0, 0.2),
     'L0_xattn_ln2_b': (0.0, 0.33),
     'L0_xattn_ln3_g': (1.0, 0.2),
     'L0_xattn_ln3_b': (0.0, 0.1),
     'L0_xattn_sa_bo': (0.0, 0.1),
     'L0_xattn_ca_bo': (0.0, 0.1),
     'L0_xattn_ff_b1': (0.0, 0.1),
     'L0_xattn_ff_b2': (0.0, 0.1)}
    factors = {}
    for name, (base, spread) in spreads.items():
        noise = np.random.default_rng([zlib.crc32(name.encode()), seed]).standard_normal(out[name].shape)
        drawn = base * np.exp(spread * noise) if base else spread * noise
        out[name] = jnp.asarray(drawn.astype(out[name].dtype))
    for name, factor in factors.items():
        out[name] = (out[name] * factor).astype(out[name].dtype)
    return out
```

```python
from contextlib import ExitStack

import concourse.bass as bass
from concourse import mybir

F32 = mybir.dt.float32
F32R = mybir.dt.float32r
ALU = mybir.AluOpType
ACT = mybir.ActivationFunctionType
AX = mybir.AxisListType

BATCH, SEQ, DM = 2, 1024, 256
DC, TC = 192, 154
HEADS, DH = 16, 64
DA = HEADS * DH
DFF = 1024
ROWS = BATCH * SEQ
P = 128
KD = DM // P
KC, PC = 2, DC // 2
HALF = 512
NBLK = ROWS // HALF
PAIRS = HEADS // 2
NPAIR = BATCH * PAIRS
EPS = 1e-5
SCALE = DH ** -0.5


class Plan:

    def __init__(self, own):
        self.own = own
        self.keys = SEQ if own else TC
        self.ks = P if own else TC // 2
        self.kt = self.keys // self.ks
        self.units = 2 * self.kt
        self.kin = KD if own else KC
        self.pin = P if own else PC
        self.kcols = [(c, min(HALF, self.keys - c)) for c in range(0, self.keys, HALF)]
        self.khalf = len(self.kcols)
        self.prep = (["K"] * self.khalf + ["Q"] * 2 + ["V"] * self.khalf + ["T"] * self.khalf + ["M"] * 2)
        self.nprep = len(self.prep)
        self.nsplit = self.khalf + 2
        self.at = {"K": 0, "Q": self.khalf, "V": self.khalf + 2, "T": 2 * self.khalf + 2, "M": 3 * self.khalf + 2}
        self.tiles = 16 * self.khalf if own else 8
        self.steps = self.order_own() if own else self.order_context()

    def order_own(self):
        nxt = {0: [("K", 0)], 1: [("K", 1)], 2: [("Q", 0)], 3: [("Q", 1)], 6: [("V", 0)], 7: [("V", 1)],
               8: [("T", 0)], 9: [("T", 1)], 12: [("M", 0)]}
        n = 0
        for u in range(5, 15):
            upto = (16 * (u - 4) + 4) // 5
            nxt.setdefault(u, [])
            nxt[u] += [("X", t) for t in range(n, upto)]
            n = upto
            if u == 9:
                nxt[u].append(("C", 0))
            if u == 14:
                nxt[u].append(("C", 1))
        out = []
        for u in range(self.units):
            if u == 0:
                out += [("M", "cur", 1), ("O", "cur", 0)]
            out.append(("S", "cur", u))
            out.append(("P", "prev", self.units - 1) if u == 0 else ("P", "cur", u - 1))
            out += {2: [("D", "prev", 1)], 4: [("Y", "prev", (1, 0))], 5: [("Y", "prev", (1, 1))],
                    10: [("D", "cur", 0)], 12: [("Y", "cur", (0, 0))], 13: [("Y", "cur", (0, 1))]}.get(u, [])
            out += [(kind, "next", a) for kind, a in nxt.get(u, [])]
            if u == 8:
                out.append(("W", "after", 0))
        return out

    def order_context(self):
        X = lambda a, b: [("X", "next", t) for t in range(a, b)]
        return [("M", "cur", 1), ("O", "cur", 0), ("S", "cur", 0), ("P", "prev", 3), ("K", "next", 0), ("Q", "next", 0),
                ("S", "cur", 1), ("P", "cur", 0), ("D", "prev", 1), ("Q", "next", 1), ("V", "next", 0), ("Y", "prev", (1, 0)),
                ("W", "after", 0),
                ("S", "cur", 2), ("P", "cur", 1), ("Y", "prev", (1, 1)), ("T", "next", 0)] + X(0, 4) + [("C", "next", 0),
                ("S", "cur", 3), ("D", "cur", 0), ("P", "cur", 2)] + X(4, 8) + [("C", "next", 1),
                ("Y", "cur", (0, 0)), ("M", "next", 0), ("Y", "cur", (0, 1))]

    def order(self, j, have):
        of = {"prev": j - 1, "cur": j, "next": j + 1, "after": j + 2}
        par = {"prev": 1, "cur": 0, "next": 1, "after": 0}
        return [(kind, of[w], a, par[w]) for kind, w, a in self.steps if w in have]

    def added(self, u):
        return (u // self.kt) * (self.kt - 1) + max(u % self.kt, 1)


SELF, CROSS = Plan(True), Plan(False)


def after(eng, sem, value):
    if not isinstance(value, int) or value > 0:
        eng.wait_ge(sem, value)


def fixed(eng, value):
    return value if isinstance(value, int) else eng.snap(value)


def bodies(eng, plan, emit):
    emit(plan.order(-1, ("next",)), 1, first=True)
    emit(plan.order(0, ("cur", "next", "after")), 0)
    with eng.Fori(1, NPAIR - 2, 2) as j:
        emit(plan.order(j, ("prev", "cur", "next", "after")), 1)
        emit(plan.order(j + 1, ("prev", "cur", "next", "after")), 0)
    emit(plan.order(NPAIR - 1, ("prev", "cur")), 1)
    emit(plan.order(NPAIR, ("prev",)), 0)


def block_kernel(nc, io, out):
    with ExitStack() as ctx:
        sem_names = {}

        def sem(name):
            sem_names[name] = ctx.enter_context(nc.semaphore(name))
            return sem_names[name]

        def sb(name, shape, dt=F32, of=ctx):
            return of.enter_context(nc.sbuf_tensor(name, shape, dt))

        xT = sb("xT", [P, KD, ROWS])
        h_hi = sb("h_hi", [P, KD, ROWS], F32R)
        h_lo = sb("h_lo", [P, KD, ROWS], F32R)
        ident = sb("ident", [P, P])
        ones = sb("ones", [P, DH])
        mean_w = sb("mean_w", [P, P])
        eps = sb("eps", [P, 1])
        NORM_V, FF_V = 3 * KD, 2 * DFF // P
        vecs = sb("vecs", [P, 3 * NORM_V + FF_V])
        vec_rows = sb("vec_rows", [3 * NORM_V + FF_V, P])
        ln_g = lambda L, k: vecs[:, L * NORM_V + k:L * NORM_V + k + 1]
        ln_b = lambda L, k: vecs[:, L * NORM_V + KD + k:L * NORM_V + KD + k + 1]
        out_b = lambda L, k: vecs[:, L * NORM_V + 2 * KD + k:L * NORM_V + 2 * KD + k + 1]
        ff_b1 = lambda f: vecs[:, 3 * NORM_V + f:3 * NORM_V + f + 1]
        psum = ctx.enter_context(nc.psum_tensor("psum", [P, 8, HALF], F32))

        attn = ExitStack()
        c_hi = sb("c_hi", [PC, KC, BATCH * TC], F32R, attn)
        c_lo = sb("c_lo", [PC, KC, BATCH * TC], F32R, attn)
        w_raw = sb("w_raw", [P, 3, KD, P], F32, attn)
        w_hi = sb("w_hi", [P, 3, KD, P], F32R, attn)
        w_lo = sb("w_lo", [P, 3, KD, P], F32R, attn)
        wo_raw = sb("wo_raw", [P, DM], F32, attn)
        wo_hi = [sb(f"wo_hi{b}", [P, DM], F32R, attn) for b in range(2)]
        wo_lo = [sb(f"wo_lo{b}", [P, DM], F32R, attn) for b in range(2)]
        kk = [sb(f"kk{b}", [P, 2, SEQ], F32R, attn) for b in range(2)]
        kl = [sb(f"kl{b}", [P, 2, SEQ], F32R, attn) for b in range(2)]
        qq = [sb(f"qq{b}", [P, 2, SEQ], F32R, attn) for b in range(2)]
        qm = [sb(f"qm{b}", [P, 2, SEQ], F32R, attn) for b in range(2)]
        val = [sb(f"val{b}", [P, SELF.kt, P], F32, attn) for b in range(2)]
        m_part = sb("m_part", [P, 2, 2, 4, 2], F32, attn)
        m_cols = [sb(f"m_cols{b}", [P, P], F32, attn) for b in range(2)]
        m_rows = [sb(f"m_rows{b}", [8, P], F32R, attn) for b in range(2)]
        late = ExitStack()
        split_hi = sb("split_hi", [P, 4, HALF], F32R, late)
        split_lo = sb("split_lo", [P, 4, HALF], F32R, late)
        valT = sb("valT", [P, 2, HALF], F32, late)
        probs = [sb(f"probs{b}", [P, 2, HALF], F32, late) for b in range(4)]
        acc = [sb(f"acc{b}", [P, 2, HALF], F32, late) for b in range(2)]
        recip = sb("recip", [P, HALF], F32, late)
        oT = sb("oT", [P, HALF], F32, late)
        o_hi = sb("o_hi", [P, HALF], F32R, late)
        o_lo = sb("o_lo", [P, HALF], F32R, late)
        late.close()
        norm = ExitStack()
        x_in = sb("x_in", [P, ROWS // P, DM], F32, norm)
        c_in = sb("c_in", [CROSS.ks, BATCH * CROSS.kt, DC], F32, norm)
        cen = [sb(f"cen{b}", [P, KD, HALF], F32, norm) for b in range(2)]
        sq = [sb(f"sq{b}", [P, KD, HALF], F32, norm) for b in range(2)]
        std = [sb(f"std{b}", [P, HALF], F32, norm) for b in range(2)]
        rstd = [sb(f"rstd{b}", [P, HALF], F32, norm) for b in range(2)]
        norm.close()
        attn.close()
        w1_raw = sb("w1_raw", [P, KD, 2 * DFF])
        w1_hi = sb("w1_hi", [P, KD, 2 * DFF], F32R)
        w1_lo = sb("w1_lo", [P, KD, 2 * DFF], F32R)
        KF = DFF // P
        w2_raw = sb("w2_raw", [P, KF, DM])
        w2_hi = sb("w2_hi", [P, KF, DM], F32R)
        w2_lo = sb("w2_lo", [P, KF, DM], F32R)
        gel = sb("gel", [P, 2, HALF])
        hid = sb("hid", [P, 2, HALF])
        hid_hi = sb("hid_hi", [P, 2, HALF], F32R)
        hid_lo = sb("hid_lo", [P, 2, HALF], F32R)
        yT = sb("yT", [P, KD, HALF])
        rows_out = sb("rows_out", [P, 4, DM])

        s_const = sem("const_set")
        s_identz = sem("ident_zeroed")
        s_klz = sem("kl_zeroed")
        s_const_v = sem("const_set_dve")
        s_vec = sem("vectors_loaded")
        s_vec_turned = sem("vectors_turned")
        s_vecs = sem("vectors_ready")
        s_x = [sem(f"x_loaded{n}") for n in range(NBLK)]
        s_ctx = sem("context_loaded")
        s_xt_ready = sem("x_turned")
        s_xt = sem("x_copied")
        s_ct_ready = sem("context_turned")
        s_ct_hi = sem("context_hi")
        s_ct = sem("context_split")
        s_mean = sem("mean_ready")
        s_cen = sem("centred")
        s_sq = sem("squared")
        s_var = sem("variance_ready")
        s_std = sem("std_ready")
        s_rstd = sem("rstd_ready")
        s_nrm = sem("normalised")
        s_aff = sem("affine_done")
        s_bias = sem("bias_added")
        s_hhi = sem("h_hi_ready")
        s_h = sem("h_ready")

        def names(pre):
            return {n: sem(f"{pre}_{n}") for n in (
                "w_loaded", "w_hi", "w_lo", "wo_loaded", "wo_hi", "wo_lo", "prep_ready", "prep_free", "split_hi",
                "moved", "x_ready", "x_read", "m_cols", "m_moved0", "m_moved1", "s_ready", "exp_done", "pv_done", "acc_done",
                "fold_ready", "fold_free", "norm_done", "o_hi", "o_lo")}

        sems = {SELF: names("self"), CROSS: names("cross")}
        s_w1 = [sem(f"ff_weights_loaded{i}") for i in range(3)]
        s_w1_hi = sem("ff_weights_hi")
        s_w1_lo = sem("ff_weights_split")
        s_gate = sem("gate_ready")
        s_lin = sem("linear_ready")
        s_gel = sem("gelu_done")
        s_hid = sem("hidden_done")
        s_hid_hi = sem("hidden_hi")
        s_hid_lo = sem("hidden_lo")
        s_y = sem("y_step")
        s_yT = sem("y_added")
        s_turn = sem("y_turned")
        s_rows = sem("rows_copied")
        s_out = sem("out_stored")

        W = {SELF: (io["sa_wq"], io["sa_wk"], io["sa_wv"], io["sa_wo"]),
             CROSS: (io["ca_wq"], io["ca_wk"], io["ca_wv"], io["ca_wo"])}
        SRC = {SELF: (h_hi, h_lo), CROSS: (c_hi, c_lo)}
        SC, PV, MX, PREP, FOLD = 0, 2, 4, 6, 7

        def cols(start, n):
            return bass.ds(start, n)

        block = ctx.enter_context(nc.Block())

        @block.sync
        def _(sp):
            for n in range(NBLK):
                t = HALF // P
                sp.dma_start(x_in[:, n * t:(n + 1) * t, :],
                             io["x"].rearrange("b (t p) d -> p (b t) d", p=P)[:, n * t:(n + 1) * t, :]).then_inc(s_x[n], 16)
            sp.dma_start(c_in[:], io["ctx"].rearrange("b (t p) d -> p (b t) d", p=CROSS.ks)).then_inc(s_ctx, 16)
            for i, (g, b, nb) in enumerate((("ln1_g", "ln1_b", "sa_bo"), ("ln2_g", "ln2_b", "ca_bo"), ("ln3_g", "ln3_b", "ff_b2"))):
                for v, name in enumerate((g, b, nb)):
                    r = i * NORM_V + v * KD
                    sp.dma_start(vec_rows[r:r + KD, :], io[name].rearrange("(k p) -> k p", p=P)).then_inc(s_vec, 16)
            sp.dma_start(vec_rows[3 * NORM_V:, :], io["ff_b1"].rearrange("(k p) -> k p", p=P)).then_inc(s_vec, 16)

            def attention(plan, h_count):
                S = sems[plan]
                wq, wk, wv, wo = W[plan]

                def load_w(J):
                    p0 = fixed(sp, (J % PAIRS) * P)
                    after(sp, S["w_lo"], J)
                    for i, w in enumerate((wq, wk, wv)):
                        n, kin = (P, KD) if i == 0 else (plan.pin, plan.kin)
                        sp.dma_start(w_raw[0:n, i, 0:kin, :],
                                     w.rearrange("(k p) c -> p k c", p=n)[:, :, cols(p0, P)]).then_inc(S["w_loaded"], 16)

                def emit(steps, par, first=False):
                    if first:
                        if plan is SELF:
                            load_w(0)
                        else:
                            sp.wait_ge(s_h, h_count)
                            load_w(0)
                        load_w(1)
                    for kind, J, a, dp in steps:
                        b = par ^ dp
                        g = plan.nprep * J + plan.at.get(kind, 0)
                        if kind == "W":
                            load_w(J)
                        elif kind == "O":
                            p0 = fixed(sp, (J % PAIRS) * P)
                            after(sp, S["wo_lo"], J)
                            sp.dma_start(wo_raw[:], wo[cols(p0, P), :]).then_inc(S["wo_loaded"], 16)
                        elif kind in ("K", "Q"):
                            split = fixed(sp, g + a + 1)
                            if kind == "K" and a == 0:
                                after(sp, S["s_ready"], 2 * plan.units * (J - 1))
                            sp.wait_ge(S["prep_free"], split)
                            s = a if kind == "K" else 2 + a
                            c0, n = plan.kcols[a] if kind == "K" else (a * HALF, HALF)
                            both, single, lo = (kk[b], kl[b], None) if kind == "K" else (qq[b], qm[b], 1)
                            own, other = slice(0, DH), slice(DH, P)
                            for h in range(2):
                                if h:
                                    own, other = other, own
                                hi_s, lo_s = split_hi[own, s, 0:n].bitcast(F32), split_lo[own, s, 0:n].bitcast(F32)
                                for dst, src in ((both[own, h, c0:c0 + n], hi_s),
                                                 (both[other, h, c0:c0 + n], lo_s if lo else hi_s),
                                                 (single[own, h, c0:c0 + n], hi_s if lo else lo_s)):
                                    sp.dma_start(dst.bitcast(F32), src).then_inc(S["moved"], 16)
                        elif kind == "M":
                            sp.wait_ge(S["prep_free"], g + a + 1)
                            for h in range(2):
                                row = DH if h == 0 else 0
                                sp.dma_start(qm[b][row:row + 1, h, a * HALF:(a + 1) * HALF].rearrange("o (t c) -> o t c", t=4).bitcast(F32),
                                             m_rows[a][4 * h:4 * h + 4, :].bitcast(F32)).then_inc(S[f"m_moved{a}"], 16)

                bodies(sp, plan, emit)

            attention(SELF, NBLK)
            attention(CROSS, 2 * NBLK)
            sp.wait_ge(s_h, 3 * NBLK)
            for k in range(KD):
                sp.dma_start(w1_raw[:, k, :], io["ff_w1"].rearrange("(k p) c -> p k c", p=P)[:, k, :]).then_inc(s_w1[k], 16)
            sp.dma_start(w2_raw[:], io["ff_w2"].rearrange("(k p) c -> p k c", p=P)).then_inc(s_w1[2], 16)
            out_v = out.rearrange("b (n t p) d -> p (b n) t d", p=P, t=4)
            with sp.Fori(0, NBLK) as n:
                for r in range(2):
                    sp.wait_ge(s_rows, 2 * n + r + 1)
                    sp.dma_start(out_v[:, cols(n, 1), 2 * r:2 * r + 2, :].rearrange("p o t d -> p (o t) d"),
                                 rows_out[:, 2 * r:2 * r + 2, :]).then_inc(s_out, 16)
            sp.wait_ge(s_out, 32 * NBLK)

        @block.tensor
        def _(pe):
            def bank(n, width=HALF):
                return psum[:, n, 0:width]

            pe.wait_ge(s_const, 1)
            for n in range(NBLK):
                pe.wait_ge(s_x[n], 16)
                for k in range(KD):
                    i = KD * n + k
                    after(pe, s_xt, i - 3)
                    for t in range(4):
                        mm = pe.transpose(psum[:, i % 4, t * P:(t + 1) * P], x_in[:, 4 * n + t, k * P:(k + 1) * P], ident[:])
                    mm.then_inc(s_xt_ready, 1)
            pe.wait_ge(s_vec, 16 * 10)
            pe.transpose(psum[:, 5, 0:3 * NORM_V + FF_V], vec_rows[:], ident[0:3 * NORM_V + FF_V, 0:3 * NORM_V + FF_V]).then_inc(s_vec_turned, 1)
            pe.wait_ge(s_ctx, 16)
            for k in range(KC):
                for t in range(BATCH * CROSS.kt):
                    mm = pe.transpose(psum[0:PC, 6 + k, t * CROSS.ks:(t + 1) * CROSS.ks],
                                      c_in[:, t, k * PC:(k + 1) * PC], ident[0:CROSS.ks, 0:CROSS.ks])
                mm.then_inc(s_ct_ready, 1)

            def normalise(L):
                if L == 0:
                    pe.wait_ge(s_xt, KD * NBLK)
                    pe.wait_ge(s_const_v, 1)
                else:
                    S = sems[SELF if L == 1 else CROSS]
                    pe.wait_ge(S["fold_free"], 6 * NPAIR)
                with pe.Fori(0, NBLK // 2) as i:
                    for u in range(2):
                        for k in range(KD):
                            mm = pe.matmul(bank(u), mean_w[:], xT[:, k, cols((2 * i + u) * HALF, HALF)],
                                           start=(k == 0), stop=(k == KD - 1))
                        mm.then_inc(s_mean, 1)
                    for u in range(2):
                        pe.wait_ge(s_sq, NBLK * L + 2 * i + u + 1)
                        for k in range(KD):
                            mm = pe.matmul(bank(2 + u), mean_w[:], sq[u][:, k, :], start=(k == 0), stop=(k == KD - 1))
                        mm.then_inc(s_var, 1)

            def attention(plan, h_count):
                S = sems[plan]
                src_hi, src_lo = SRC[plan]

                def project(which, src, kin, pin, c0, n):
                    hi, lo = src
                    for k in range(kin):
                        a_hi, a_lo = w_hi[0:pin, which, k, :], w_lo[0:pin, which, k, :]
                        x_hi, x_lo = hi[0:pin, k, cols(c0, n)], lo[0:pin, k, cols(c0, n)]
                        for m, (w, x) in enumerate(((a_hi, x_hi), (a_hi, x_lo), (a_lo, x_hi))):
                            mm = pe.matmul(bank(PREP, n), w, x, start=(k == 0 and m == 0), stop=(k == kin - 1 and m == 2))
                    return mm

                def emit(steps, par, first=False):
                    if first:
                        pe.wait_ge(s_h, h_count)
                        pe.wait_ge(s_const_v, 3)
                        if plan is CROSS:
                            pe.wait_ge(s_ct, KC)
                    for kind, J, a, dp in steps:
                        b = par ^ dp
                        g = plan.nprep * J + plan.at.get(kind, 0)
                        if kind in "KQV":
                            if kind == "K" and a == 0:
                                pe.wait_ge(S["w_lo"], J + 1)
                            after(pe, S["prep_free"], g + a)
                            if kind == "Q":
                                mm = project(0, (h_hi, h_lo), KD, P, (J // PAIRS) * SEQ + a * HALF, HALF)
                            else:
                                c0, n = plan.kcols[a]
                                mm = project(1 if kind == "K" else 2, (src_hi, src_lo), plan.kin, plan.pin,
                                             (J // PAIRS) * plan.keys + c0, n)
                            mm.then_inc(S["prep_ready"], 1)
                        elif kind == "T":
                            pe.wait_ge(S["prep_free"], g + a)
                            n = plan.kt // plan.khalf
                            for t in range(n):
                                mm = pe.transpose(psum[0:plan.ks, PREP, t * P:(t + 1) * P],
                                                  valT[:, a, t * plan.ks:(t + 1) * plan.ks], ident[:])
                            mm.then_inc(S["prep_ready"], 1)
                        elif kind == "X":
                            n = plan.tiles * J + a
                            if a == 0:
                                pe.wait_ge(S["moved"], 96 * plan.nsplit * (J + 1))
                            after(pe, S["x_read"], n - 1)
                            if plan.khalf == 2:
                                half, h, t, kh = a // 16, a // 2 % 2, a // 4 % 4, a % 2
                                q0 = half * HALF + t * P
                                mm = pe.matmul(bank(MX + a % 2), qq[b][:, h, q0:q0 + P], kk[b][:, h, kh * HALF:(kh + 1) * HALF],
                                               start=True, stop=True)
                            else:
                                for h in range(2):
                                    mm = pe.matmul(psum[:, MX + a % 2, h * plan.keys:(h + 1) * plan.keys],
                                                   qq[b][:, h, a * P:(a + 1) * P], kk[b][:, h, 0:plan.keys], start=True, stop=True)
                            mm.then_inc(S["x_ready"], 1)
                        elif kind == "M":
                            pe.wait_ge(S["m_cols"], 2 * J + a + 1)
                            pe.wait_ge(S["prep_free"], g + a)
                            pe.transpose(psum[:, PREP, 0:P], m_cols[a][:], ident[:]).then_inc(S["prep_ready"], 1)
                        elif kind == "S":
                            half, kt = a // plan.kt, a % plan.kt
                            if kt == 0:
                                pe.wait_ge(S[f"m_moved{half}"], 32 * (J + 1))
                            ks = slice(kt * plan.ks, (kt + 1) * plan.ks)
                            qs = slice(half * HALF, (half + 1) * HALF)
                            for h in range(2):
                                after(pe, S["exp_done"], 2 * plan.units * J + 2 * a + h - 1)
                                pe.matmul(psum[0:plan.ks, SC + h, :], kk[b][:, h, ks], qq[b][:, h, qs], start=True, stop=False)
                                pe.matmul(psum[0:plan.ks, SC + h, :], kl[b][:, h, ks], qm[b][:, h, qs],
                                          start=False, stop=True).then_inc(S["s_ready"], 1)
                        elif kind == "P":
                            half, kt = a // plan.kt, a % plan.kt
                            if kt == 0:
                                after(pe, S["norm_done"], 2 * J + half - 1)
                            pe.wait_ge(S["exp_done"], 2 * plan.units * J + 2 * a + 2)
                            for h in range(2):
                                d = slice(h * DH, (h + 1) * DH)
                                mm = pe.matmul(psum[d, PV + half, :], val[b][0:plan.ks, kt, d], probs[a % 4][0:plan.ks, h, :],
                                               start=(kt == 0), stop=(kt == plan.kt - 1))
                            mm.then_inc(S["pv_done"], 1)
                        elif kind == "D":
                            pe.wait_ge(S["acc_done"], (plan.kt - 1) * (2 * J + a + 1))
                            after(pe, S["fold_free"], 6 * J + 3 * a)
                            for h in range(2):
                                mm = pe.matmul(psum[h * DH:(h + 1) * DH, FOLD, :], ones[0:plan.ks, :], acc[a][0:plan.ks, h, :],
                                               start=True, stop=True)
                            mm.then_inc(S["fold_ready"], 1)
                        elif kind == "Y":
                            half, m = a
                            if m == 0:
                                pe.wait_ge(S["o_lo"], 2 * J + half + 1)
                                pe.wait_ge(S["wo_lo"], J + 1)
                            pe.wait_ge(S["fold_free"], 6 * J + 3 * half + 1 + m)
                            mc = slice(m * P, (m + 1) * P)
                            pe.matmul(bank(FOLD), wo_hi[b][:, mc], o_hi[:], start=True, stop=False)
                            pe.matmul(bank(FOLD), wo_hi[b][:, mc], o_lo[:], start=False, stop=False)
                            pe.matmul(bank(FOLD), wo_lo[b][:, mc], o_hi[:], start=False, stop=True).then_inc(S["fold_ready"], 1)

                bodies(pe, plan, emit)

            def feed_forward():
                def turn(n):
                    pe.wait_ge(s_yT, n + 1)
                    after(pe, s_rows, 2 * n)
                    for t in range(4):
                        for m in range(KD):
                            mm = pe.transpose(psum[:, 6 + t // 2, (t % 2) * DM + m * P:(t % 2) * DM + (m + 1) * P],
                                              yT[:, m, t * P:(t + 1) * P], ident[:])
                        if t % 2:
                            mm.then_inc(s_turn, 1)

                def down(n, f):
                    q = KF * n + f
                    if f == 0:
                        after(pe, s_yT, n)
                    pe.wait_ge(s_hid_lo, q + 1)
                    for m in range(KD):
                        mc = slice(m * P, (m + 1) * P)
                        for i, (w, x) in enumerate(((w2_hi, hid_hi), (w2_hi, hid_lo), (w2_lo, hid_hi))):
                            mm = pe.matmul(bank(4 + m), w[:, f, mc], x[:, f % 2, :], start=(f == 0 and i == 0),
                                           stop=(f == KF - 1 and i == 2))
                    mm.then_inc(s_y, 1)

                def one(n, tail):
                    for f in range(KF):
                        q = KF * n + f
                        for c, bk, ready, read in ((DFF + f * P, 2 + f % 2, s_gate, s_gel), (f * P, f % 2, s_lin, s_hid)):
                            after(pe, read, q - 1)
                            for k in range(KD):
                                for i, (w, x) in enumerate(((w1_hi, h_hi), (w1_hi, h_lo), (w1_lo, h_hi))):
                                    mm = pe.matmul(bank(bk), w[:, k, c:c + P], x[:, k, cols(n * HALF, HALF)],
                                                   start=(k == 0 and i == 0), stop=(k == KD - 1 and i == 2))
                            mm.then_inc(ready, 1)
                        if f:
                            down(n, f - 1)
                        if f == 2 and tail:
                            turn(n - 1)
                    down(n, KF - 1)

                pe.wait_ge(s_w1_lo, 3)
                pe.wait_ge(s_h, 3 * NBLK)
                one(0, False)
                with pe.Fori(1, NBLK) as n:
                    one(n, True)
                turn(NBLK - 1)

            normalise(0)
            attention(SELF, NBLK)
            normalise(1)
            attention(CROSS, 2 * NBLK)
            normalise(2)
            feed_forward()

        @block.vector
        def _(dve):
            dve.memset(mean_w[:], 1.0 / DM)
            dve.memset(eps[:], EPS)
            dve.memset(ones[:], 1.0).then_inc(s_const_v, 1)
            for b in range(2):
                dve.memset(m_cols[b][:], 0.0)
                dve.memset(qm[b][:].bitcast(F32), 0.0)
                dve.memset(kl[b][:].bitcast(F32), 0.0).then_inc(s_klz, 1)
                dve.wait_ge(s_klz, b + 1)
                dve.memset(kl[b][DH:DH + 1, 0, :].bitcast(F32), -1.0)
                dve.memset(kl[b][0:1, 1, :].bitcast(F32), -1.0).then_inc(s_const_v, 1)
            for n in range(NBLK):
                for k in range(KD):
                    i = KD * n + k
                    dve.wait_ge(s_xt_ready, i + 1)
                    dve.tensor_copy(xT[:, k, n * HALF:(n + 1) * HALF], psum[:, i % 4, :]).then_inc(s_xt, 1)
            dve.wait_ge(s_vec_turned, 1)
            dve.tensor_copy(vecs[:], psum[:, 5, 0:3 * NORM_V + FF_V]).then_inc(s_vecs, 1)
            for k in range(KC):
                dve.wait_ge(s_ct_hi, k + 1)
                dve.tensor_tensor(c_lo[:, k, :], psum[0:PC, 6 + k, 0:BATCH * TC], c_hi[:, k, :], ALU.subtract).then_inc(s_ct, 1)

            def normalise(L):
                if L == 0:
                    dve.wait_ge(s_vecs, 1)
                with dve.Fori(0, NBLK // 2) as i:
                    blk = [cols((2 * i + u) * HALF, HALF) for u in range(2)]
                    for u in range(2):
                        n = NBLK * L + 2 * i + u + 1
                        dve.wait_ge(s_mean, n)
                        dve.tensor_tensor(cen[u][:], xT[:, :, blk[u]], psum[:, u, :].unsqueeze(1).to_broadcast([P, KD, HALF]),
                                          ALU.subtract).then_inc(s_cen, 1)
                    for u in range(2):
                        dve.wait_ge(s_cen, NBLK * L + 2 * i + u + 1)
                        for k in range(KD):
                            dve.tensor_scalar(xT[:, k, blk[u]], xT[:, k, blk[u]], out_b(L, k), None,
                                              ALU.add).then_inc(s_bias, 1)
                    for u in range(2):
                        n = NBLK * L + 2 * i + u + 1
                        dve.wait_ge(s_std, n)
                        dve.reciprocal(rstd[u][:], std[u][:]).then_inc(s_rstd, 1)
                        dve.wait_ge(s_rstd, n)
                        dve.tensor_tensor(cen[u][:], cen[u][:], rstd[u][:].unsqueeze(1).to_broadcast([P, KD, HALF]),
                                          ALU.mult).then_inc(s_nrm, 1)
                        dve.wait_ge(s_nrm, n)
                        for k in range(KD):
                            dve.tensor_scalar(sq[u][:, k, :], cen[u][:, k, :], ln_g(L, k), ln_b(L, k),
                                              ALU.mult, ALU.add).then_inc(s_aff, 1)
                    for u in range(2):
                        n = NBLK * L + 2 * i + u + 1
                        dve.wait_ge(s_hhi, n)
                        dve.tensor_tensor(h_lo[:, :, blk[u]], sq[u][:], h_hi[:, :, blk[u]], ALU.subtract).then_inc(s_h, 1)

            def attention(plan, h_count):
                S = sems[plan]

                def emit(steps, par, first=False):
                    if first:
                        dve.wait_ge(s_h, h_count)
                        dve.wait_ge(s_bias, 2 * h_count)
                    for kind, J, a, dp in steps:
                        g = plan.nprep * J + plan.at.get(kind, 0)
                        if kind in "KQ":
                            s = a if kind == "K" else 2 + a
                            n = plan.kcols[a][1] if kind == "K" else HALF
                            dve.wait_ge(S["split_hi"], plan.nsplit * J + plan.at[kind] + a + 1)
                            dve.tensor_tensor(split_lo[:, s, 0:n], psum[:, PREP, 0:n], split_hi[:, s, 0:n],
                                              ALU.subtract).then_inc(S["prep_free"], 1)
                        elif kind == "X":
                            dve.wait_ge(S["x_ready"], plan.tiles * J + a + 1)
                            if plan.khalf == 2:
                                half, h, t, kh = a // 16, a // 2 % 2, a // 4 % 4, a % 2
                                dve.tensor_reduce(m_part[:, half, h, t, kh:kh + 1], psum[:, MX + a % 2, :], AX.X,
                                                  ALU.max).then_inc(S["x_read"], 1)
                            else:
                                dve.tensor_reduce(m_part[:, a // 4, :, a % 4, 0],
                                                  psum[:, MX + a % 2, 0:2 * plan.keys].rearrange("p (h k) -> p h k", h=2),
                                                  AX.X, ALU.max).then_inc(S["x_read"], 1)
                        elif kind == "C":
                            dve.wait_ge(S["x_read"], plan.tiles * J + plan.tiles // 2 * (a + 1))
                            dve.tensor_reduce(m_cols[a][:, 0:8], m_part[:, a, :, :, 0:plan.khalf].rearrange("p h t k -> p (h t) k"),
                                              AX.X, ALU.max).then_inc(S["m_cols"], 1)
                        elif kind == "M":
                            after(dve, S[f"m_moved{a}"], 32 * J)
                            dve.wait_ge(S["prep_ready"], g + a + 1)
                            dve.tensor_copy(m_rows[a][:], psum[0:8, PREP, 0:P]).then_inc(S["prep_free"], 1)
                        elif kind == "D":
                            f = 6 * J + 3 * a + 1
                            dve.wait_ge(S["fold_ready"], f)
                            dve.reciprocal(recip[:], psum[:, FOLD, :]).then_inc(S["fold_free"], 1)
                            dve.wait_ge(S["fold_free"], f)
                            dve.wait_ge(S["pv_done"], plan.units * J + plan.kt * (a + 1))
                            after(dve, S["o_lo"], 2 * J + a)
                            dve.tensor_tensor(oT[:], psum[:, PV + a, :], recip[:], ALU.mult).then_inc(S["norm_done"], 1)
                        elif kind == "Y":
                            half, m = a
                            dve.wait_ge(S["fold_ready"], 6 * J + 3 * half + 2 + m)
                            x = xT[:, m, cols((J // PAIRS) * SEQ + half * HALF, HALF)]
                            dve.tensor_tensor(x, x, psum[:, FOLD, :], ALU.add).then_inc(S["fold_free"], 1)

                bodies(dve, plan, emit)

            def feed_forward():
                dve.wait_ge(s_w1_hi, 1)
                dve.tensor_tensor(w1_lo[:, 0, :], w1_raw[:, 0, :], w1_hi[:, 0, :], ALU.subtract).then_inc(s_w1_lo, 1)
                dve.wait_ge(s_w1_hi, 2)
                dve.tensor_tensor(w1_lo[:, 1, :], w1_raw[:, 1, :], w1_hi[:, 1, :], ALU.subtract).then_inc(s_w1_lo, 1)
                dve.wait_ge(s_w1_hi, 3)
                dve.tensor_tensor(w2_lo[:], w2_raw[:], w2_hi[:], ALU.subtract).then_inc(s_w1_lo, 1)

                def lo(n, f):
                    q = KF * n + f
                    dve.wait_ge(s_hid_hi, q + 1)
                    dve.tensor_tensor(hid_lo[:, f % 2, :], hid[:, f % 2, :], hid_hi[:, f % 2, :], ALU.subtract).then_inc(s_hid_lo, 1)

                def one(n):
                    for f in range(KF):
                        q = KF * n + f
                        dve.wait_ge(s_gel, q + 1)
                        dve.wait_ge(s_lin, q + 1)
                        if f >= 2 or not isinstance(n, int):
                            after(dve, s_hid_lo, q - 1)
                        dve.scalar_tensor_tensor(hid[:, f % 2, :], psum[:, f % 2, :], ff_b1(f), gel[:, f % 2, :],
                                                 ALU.add, ALU.mult).then_inc(s_hid, 1)
                        if f:
                            lo(n, f - 1)
                    lo(n, KF - 1)
                    dve.wait_ge(s_y, KF * (n + 1))
                    after(dve, s_turn, 2 * n)
                    dve.tensor_tensor(yT[:], psum[:, 4:6, :], xT[:, :, cols(n * HALF, HALF)], ALU.add).then_inc(s_yT, 1)

                one(0)
                with dve.Fori(1, NBLK) as n:
                    one(n)

            normalise(0)
            attention(SELF, NBLK)
            normalise(1)
            attention(CROSS, 2 * NBLK)
            normalise(2)
            feed_forward()

        @block.scalar
        def _(act):
            for k in range(KC):
                act.wait_ge(s_ct_ready, k + 1)
                act.activation(c_hi[:, k, :], psum[0:PC, 6 + k, 0:BATCH * TC], ACT.Copy).then_inc(s_ct_hi, 1)

            def normalise(L):
                if L == 0:
                    act.wait_ge(s_const_v, 1)
                with act.Fori(0, NBLK // 2) as i:
                    for u in range(2):
                        act.wait_ge(s_cen, NBLK * L + 2 * i + u + 1)
                        act.activation(sq[u][:], cen[u][:], ACT.Square).then_inc(s_sq, 1)
                    for u in range(2):
                        act.wait_ge(s_var, NBLK * L + 2 * i + u + 1)
                        act.activation(std[u][:], psum[:, 2 + u, :], ACT.Sqrt, bias=eps[:]).then_inc(s_std, 1)
                    for u in range(2):
                        act.wait_ge(s_aff, KD * (NBLK * L + 2 * i + u + 1))
                        act.activation(h_hi[:, :, cols((2 * i + u) * HALF, HALF)], sq[u][:], ACT.Copy).then_inc(s_hhi, 1)

            def attention(plan, h_count):
                S = sems[plan]

                def split_w(J):
                    act.wait_ge(S["w_loaded"], 48 * (J + 1))
                    after(act, S["prep_ready"], plan.nprep * (J - 1) + plan.at["T"])
                    if plan is SELF:
                        act.activation(w_hi[:], w_raw[:], ACT.Copy).then_inc(S["w_hi"], 1)
                    else:
                        act.activation(w_hi[:, 0, :, :], w_raw[:, 0, :, :], ACT.Copy).then_inc(S["w_hi"], 1)
                        act.activation(w_hi[0:PC, 1:3, :, :], w_raw[0:PC, 1:3, :, :], ACT.Copy).then_inc(S["w_hi"], 1)

                def emit(steps, par, first=False):
                    if first:
                        split_w(0)
                    for kind, J, a, dp in steps:
                        b = par ^ dp
                        g = plan.nprep * J + plan.at.get(kind, 0)
                        if kind == "W":
                            split_w(J)
                        elif kind == "O":
                            act.wait_ge(S["wo_loaded"], 16 * (J + 1))
                            after(act, S["fold_ready"], 6 * (J - 1))
                            act.activation(wo_hi[b][:], wo_raw[:], ACT.Copy).then_inc(S["wo_hi"], 1)
                        elif kind in "KQ":
                            s = a if kind == "K" else 2 + a
                            n = plan.kcols[a][1] if kind == "K" else HALF
                            act.wait_ge(S["prep_ready"], g + a + 1)
                            if a == 0:
                                after(act, S["moved"], 96 * plan.nsplit * J)
                            act.activation(split_hi[:, s, 0:n], psum[:, PREP, 0:n], ACT.Copy).then_inc(S["split_hi"], 1)
                        elif kind == "V":
                            act.wait_ge(S["prep_ready"], g + a + 1)
                            n = plan.kcols[a][1]
                            act.activation(valT[:, a, 0:n], psum[:, PREP, 0:n], ACT.Copy).then_inc(S["prep_free"], 1)
                        elif kind == "T":
                            act.wait_ge(S["prep_ready"], g + a + 1)
                            n = plan.kt // plan.khalf
                            act.activation(val[b][0:plan.ks, a * n:(a + 1) * n, :],
                                           psum[0:plan.ks, PREP, 0:n * P].rearrange("p (t d) -> p t d", t=n),
                                           ACT.Copy).then_inc(S["prep_free"], 1)
                        elif kind == "S":
                            for h in range(2):
                                if h == 0:
                                    after(act, S["pv_done"], plan.units * J + a - 3)
                                    back = a - 4
                                    if back < 0:
                                        back += plan.units
                                        after(act, S["acc_done"], 2 * (plan.kt - 1) * (J - 1) + plan.added(back))
                                    else:
                                        after(act, S["acc_done"], 2 * (plan.kt - 1) * J + plan.added(back))
                                act.wait_ge(S["s_ready"], 2 * plan.units * J + 2 * a + h + 1)
                                act.activation(probs[a % 4][0:plan.ks, h, :], psum[0:plan.ks, SC + h, :], ACT.Exp,
                                               scale=SCALE).then_inc(S["exp_done"], 1)
                        elif kind == "D":
                            act.wait_ge(S["norm_done"], 2 * J + a + 1)
                            after(act, S["fold_ready"], 6 * J + 3 * a)
                            act.activation(o_hi[:], oT[:], ACT.Copy).then_inc(S["o_hi"], 1)

                def emit_w1(steps, par, first=False):
                    emit(steps, par, first)
                    if first:
                        split_w(1)

                bodies(act, plan, emit_w1)

            def feed_forward():
                act.wait_ge(s_vecs, 1)
                act.wait_ge(s_w1[0], 16)
                act.activation(w1_hi[:, 0, :], w1_raw[:, 0, :], ACT.Copy).then_inc(s_w1_hi, 1)
                act.wait_ge(s_w1[1], 16)
                act.activation(w1_hi[:, 1, :], w1_raw[:, 1, :], ACT.Copy).then_inc(s_w1_hi, 1)
                act.wait_ge(s_w1[2], 16)
                act.activation(w2_hi[:], w2_raw[:], ACT.Copy).then_inc(s_w1_hi, 1)

                def hi(n, f):
                    q = KF * n + f
                    act.wait_ge(s_hid, q + 1)
                    after(act, s_y, q - 1)
                    act.activation(hid_hi[:, f % 2, :], hid[:, f % 2, :], ACT.Copy).then_inc(s_hid_hi, 1)

                def store(n):
                    for r in range(2):
                        act.wait_ge(s_turn, 2 * n + r + 1)
                        after(act, s_out, 32 * n)
                        act.activation(rows_out[:, 2 * r:2 * r + 2, :],
                                       psum[:, 6 + r, :].rearrange("p (t d) -> p t d", t=2), ACT.Copy).then_inc(s_rows, 1)

                def one(n, tail):
                    for f in range(KF):
                        q = KF * n + f
                        act.wait_ge(s_gate, q + 1)
                        after(act, s_hid, q - 1)
                        act.activation(gel[:, f % 2, :], psum[:, 2 + f % 2, :], ACT.Gelu,
                                       bias=ff_b1(KF + f)).then_inc(s_gel, 1)
                        if f:
                            hi(n, f - 1)
                        if f == 3 and tail:
                            store(n - 1)
                    hi(n, KF - 1)

                one(0, False)
                with act.Fori(1, NBLK) as n:
                    one(n, True)
                store(NBLK - 1)

            normalise(0)
            attention(SELF, NBLK)
            normalise(1)
            attention(CROSS, 2 * NBLK)
            normalise(2)
            feed_forward()

        @block.gpsimd
        def _(pool):
            pool.memset(ident[:], 0.0).then_inc(s_identz, 1)
            pool.wait_ge(s_identz, 1)
            pool.affine_select(out=ident[:], in_=ident[:], compare_op=ALU.not_equal, fill=1.0, base=0,
                               pattern=[[-1, P]], channel_multiplier=1).then_inc(s_const, 1)
            def attention(plan, h_count):
                S = sems[plan]

                def split_w(J):
                    if plan is SELF:
                        pool.wait_ge(S["w_hi"], J + 1)
                        pool.tensor_tensor(w_lo[:], w_raw[:], w_hi[:], ALU.subtract).then_inc(S["w_lo"], 1)
                    else:
                        pool.wait_ge(S["w_hi"], 2 * J + 2)
                        pool.tensor_tensor(w_lo[:, 0, :, :], w_raw[:, 0, :, :], w_hi[:, 0, :, :], ALU.subtract)
                        pool.tensor_tensor(w_lo[0:PC, 1:3, :, :], w_raw[0:PC, 1:3, :, :], w_hi[0:PC, 1:3, :, :],
                                           ALU.subtract).then_inc(S["w_lo"], 1)

                def emit(steps, par, first=False):
                    if first:
                        split_w(0)
                    for kind, J, a, dp in steps:
                        b = par ^ dp
                        if kind == "W":
                            split_w(J)
                        elif kind == "O":
                            pool.wait_ge(S["wo_hi"], J + 1)
                            pool.tensor_tensor(wo_lo[b][:], wo_raw[:], wo_hi[b][:], ALU.subtract).then_inc(S["wo_lo"], 1)
                        elif kind == "S":
                            half, kt = a // plan.kt, a % plan.kt
                            if kt == 0:
                                continue
                            now, last = probs[a % 4][0:plan.ks], probs[(a - 1) % 4][0:plan.ks]
                            total = acc[half][0:plan.ks]
                            if kt == 1:
                                after(pool, S["fold_ready"], 6 * (J - 1) + 3 * half + 1)
                            else:
                                pool.wait_ge(S["acc_done"], 2 * (plan.kt - 1) * J + plan.added(a) - 1)
                            pool.wait_ge(S["exp_done"], 2 * plan.units * J + 2 * a + 2)
                            pool.tensor_tensor(total, last if kt == 1 else total, now, ALU.add).then_inc(S["acc_done"], 1)
                        elif kind == "D":
                            pool.wait_ge(S["o_hi"], 2 * J + a + 1)
                            pool.tensor_tensor(o_lo[:], oT[:], o_hi[:], ALU.subtract).then_inc(S["o_lo"], 1)

                def emit_w1(steps, par, first=False):
                    emit(steps, par, first)
                    if first:
                        split_w(1)

                bodies(pool, plan, emit_w1)

            attention(SELF, NBLK)
            attention(CROSS, 2 * NBLK)


_NAMES = {"x": "x", "ctx_768": "ctx"}
_PREFIX = "L0_xattn_"
_INS = ["x", "ctx_768"] + [_PREFIX + n for n in (
    "ln1_g", "ln1_b", "ln2_g", "ln2_b", "ln3_g", "ln3_b", "sa_wq", "sa_wk", "sa_wv", "sa_wo", "sa_bo",
    "ca_wq", "ca_wk", "ca_wv", "ca_wo", "ca_bo", "ff_w1", "ff_b1", "ff_w2", "ff_b2")]


def kernel(**inputs):
    import numpy as _np
    import concourse.bacc as _bacc
    from concourse import mybir as _mybir
    from concourse.bass_utils import run_bass_kernel_spmd as _run

    nc = _bacc.Bacc("TRN2", target_bir_lowering=False, num_devices=1)
    arrays, io = {}, {}
    for name in _INS:
        a = _np.ascontiguousarray(inputs[name])
        arrays[f"in_{name}"] = a
        io[_NAMES.get(name, name.removeprefix(_PREFIX))] = nc.dram_tensor(
            f"in_{name}", a.shape, _mybir.dt.from_np(a.dtype), kind="ExternalInput").ap()
    out = nc.dram_tensor("out", (BATCH, SEQ, DM), _mybir.dt.float32, kind="ExternalOutput").ap()
    block_kernel(nc, io, out)
    r = _run(nc, [arrays], core_ids=[0])
    return r.results[0]["out"]
```

```python
from contextlib import ExitStack

import concourse.bass as bass
from concourse import mybir

F32 = mybir.dt.float32
F32R = mybir.dt.float32r
ALU = mybir.AluOpType
ACT = mybir.ActivationFunctionType
AX = mybir.AxisListType

BATCH, SEQ, DM = 2, 1024, 256
DC, TC = 192, 154
HEADS, DH = 16, 64
DA = HEADS * DH
DFF = 1024
ROWS = BATCH * SEQ
P = 128
KD = DM // P
KC, PC = 2, DC // 2
HALF = 512
NBLK = ROWS // HALF
QUAD = P // NBLK
PAIRS = HEADS // 2
NPAIR = BATCH * PAIRS
EPS = 1e-5
SCALE = DH ** -0.5


ENGINES = ("sp", "pe", "dve", "act", "pool")
CROSS_ORDER = {
    "sp": "M0 W++ M1 L",
    "pe": "K+ Q0+ D1- S0.1 S1.0 Q1+ V+ X0+ S1.1 X1+ Y0.0- X2+ S2.0 X3+ T+ S2.1 X4+ Y0.1- S3.0 X5+ S3.1 M0+ X6+ D0 "
          "P0 P1 P2 X7+ S0.0+ Y1.0- P3 M1+ Y1.1-",
    "dve": "K+ R0- D1- X0+ X1+ X2+ Y0.0- X3+ C0+ X4+ Y0.1- X5+ M0+ R1- X6+ D0 X7+ C1+ Y1.0- M1+ Y1.1-",
    "act": "B1 K+ Q0+ S0.1 N0- Q1+ V+ S1.0 B0+ S1.1 S2.0 W++ S2.1 N1- S3.0 S3.1 O S0.0+ T+",
    "pool": "S3.1- Q0+ N0- Q1+ S1.1 N1- O W++",
}


def read_order(text):
    which = {"-": "prev", "": "cur", "+": "next", "++": "after"}
    out = []
    for word in text.split():
        name = word.rstrip("+-")
        args = tuple(int(n) for n in name[1:].split(".")) if name[1:] else (0,)
        out.append((name[0], which[word[len(name):]], args if len(args) == 2 else args[0]))
    return out


class Plan:

    def __init__(self, own):
        self.own = own
        self.keys = SEQ if own else TC
        self.ks = P if own else TC // 2
        self.kt = self.keys // self.ks
        self.units = 2 * self.kt
        self.kin = KD if own else KC
        self.pin = P if own else PC
        self.kcols = [(c, min(HALF, self.keys - c)) for c in range(0, self.keys, HALF)]
        self.khalf = len(self.kcols)
        self.prep = (["K"] * self.khalf + ["Q"] * 2 + ["V"] * self.khalf + ["T"] * self.khalf + ["M"] * 2)
        self.nprep = len(self.prep)
        self.nsplit = self.khalf + 2
        self.at = {"K": 0, "Q": self.khalf, "V": self.khalf + 2, "T": 2 * self.khalf + 2, "M": 3 * self.khalf + 2}
        self.tiles = 16 * self.khalf if own else 8
        self.pv_banks, self.mx_banks, self.prep_banks = (2, 2, 1) if own else (2, 1, 2)
        self.steps = dict.fromkeys(ENGINES, self.order_own()) if own else {e: read_order(t) for e, t in CROSS_ORDER.items()}

    def order_own(self):
        first = {0: [("M", "cur", 1), ("O", "cur", 0)]}
        extra = {0: [("N", "prev", 0), ("K", "next", 0)], 1: [("K", "next", 1)],
                 2: [("D", "prev", 1), ("R", "prev", 1), ("Q", "next", 0), ("B", "next", 0)],
                 3: [("Q", "next", 1), ("B", "next", 1)], 4: [("Y", "prev", (0, 0)), ("V", "next", 0)],
                 5: [("Y", "prev", (0, 1)), ("V", "next", 1)], 6: [("N", "prev", 1), ("T", "next", 0)],
                 7: [("T", "next", 1)], 8: [("W", "after", 0), ("L", "next", 0)], 9: [("C", "next", 0)], 11: [("M", "next", 0)],
                 13: [("C", "next", 1), ("D", "cur", 0), ("R", "cur", 0)], 14: [("Y", "prev", (1, 0))], 15: [("Y", "prev", (1, 1))]}
        out = []
        for u in range(self.units):
            x = [("X", "next", 4 * (u - 6) + i) for i in range(4)] if 6 <= u < 14 else []
            out += first.get(u, []) + [("S", "cur", (u, 0))] + x[0:1] + [("S", "cur", (u, 1))] + x[1:2]
            out += [("P", "prev", self.units - 1) if u == 0 else ("P", "cur", u - 1)] + x[2:4] + extra.get(u, [])
        return out

    def order(self, engine, j, have):
        of = {"prev": j - 1, "cur": j, "next": j + 1, "after": j + 2}
        par = {"prev": 1, "cur": 0, "next": 1, "after": 0}
        return [(kind, of[w], a, par[w]) for kind, w, a in self.steps[engine] if w in have]

    def added(self, u):
        return (u // self.kt) * (self.kt - 1) + max(u % self.kt, 1)


SELF, CROSS = Plan(True), Plan(False)


def after(eng, sem, value):
    if not isinstance(value, int) or value > 0:
        eng.wait_ge(sem, value)


def fixed(eng, value):
    return value if isinstance(value, int) else eng.snap(value)


def bodies(engine, eng, plan, emit):
    emit(plan.order(engine, -2, ("after",)), 0)
    emit(plan.order(engine, -1, ("next", "after")), 1)
    emit(plan.order(engine, 0, ("cur", "next", "after")), 0)
    emit(plan.order(engine, 1, ("prev", "cur", "next", "after")), 1)
    with eng.Fori(2, NPAIR - 3, 2) as j:
        emit(plan.order(engine, j, ("prev", "cur", "next", "after")), 0)
        emit(plan.order(engine, j + 1, ("prev", "cur", "next", "after")), 1)
    emit(plan.order(engine, NPAIR - 2, ("prev", "cur", "next")), 0)
    emit(plan.order(engine, NPAIR - 1, ("prev", "cur")), 1)
    emit(plan.order(engine, NPAIR, ("prev",)), 0)


def block_kernel(nc, io, out):
    with ExitStack() as ctx:
        sem_names = {}

        def sem(name):
            sem_names[name] = ctx.enter_context(nc.semaphore(name))
            return sem_names[name]

        def sb(name, shape, dt=F32, of=ctx):
            return of.enter_context(nc.sbuf_tensor(name, shape, dt))

        xT = sb("xT", [P, KD, ROWS])
        h_hi = sb("h_hi", [P, KD, ROWS], F32R)
        h_lo = sb("h_lo", [P, KD, ROWS], F32R)
        ident = sb("ident", [P, P])
        ones = sb("ones", [P, DH])
        mean_w = sb("mean_w", [P, P])
        eps = sb("eps", [P, 1])
        pick = sb("pick", [P, NBLK, P])
        NORM_V, FF_V = 3 * KD, 2 * DFF // P
        vecs = sb("vecs", [P, 3 * NORM_V + FF_V])
        vec_rows = sb("vec_rows", [3 * NORM_V + FF_V, P])
        ln_g = lambda L, k: vecs[:, L * NORM_V + k:L * NORM_V + k + 1]
        ln_b = lambda L, k: vecs[:, L * NORM_V + KD + k:L * NORM_V + KD + k + 1]
        out_b = lambda L, k: vecs[:, L * NORM_V + 2 * KD + k:L * NORM_V + 2 * KD + k + 1]
        ff_b1 = lambda f: vecs[:, 3 * NORM_V + f:3 * NORM_V + f + 1]
        psum = ctx.enter_context(nc.psum_tensor("psum", [P, 8, HALF], F32))

        attn = ExitStack()
        keys_hh, keys_lm = {}, {}
        for plan, of in ((SELF, "self"), (CROSS, "cross")):
            keys_hh[plan] = [sb(f"{of}_keys_hh{b}", [P, 2, plan.keys], F32R, attn) for b in range(2)]
            keys_lm[plan] = [sb(f"{of}_keys_lm{b}", [P, 2, plan.keys], F32R, attn) for b in range(2)]
        c_hi = sb("c_hi", [PC, KC, BATCH * TC], F32R, attn)
        c_lo = sb("c_lo", [PC, KC, BATCH * TC], F32R, attn)
        w_raw = sb("w_raw", [P, 3, KD, P], F32, attn)
        w_hi = sb("w_hi", [P, 3, KD, P], F32R, attn)
        w_lo = sb("w_lo", [P, 3, KD, P], F32R, attn)
        wo_raw = sb("wo_raw", [P, DM], F32, attn)
        wo_hi = [sb(f"wo_hi{b}", [P, DM], F32R, attn) for b in range(2)]
        wo_lo = [sb(f"wo_lo{b}", [P, DM], F32R, attn) for b in range(2)]
        qq = [sb(f"qq{b}", [P, 2, SEQ], F32R, attn) for b in range(2)]
        qm = [sb(f"qm{b}", [P, 2, SEQ], F32R, attn) for b in range(2)]
        val = [sb(f"val{b}", [P, SELF.kt, P], F32, attn) for b in range(2)]
        m_part = sb("m_part", [P, 2, 2, 4, 2], F32, attn)
        m_cols = [sb(f"m_cols{b}", [P, P], F32, attn) for b in range(2)]
        m_rows = [sb(f"m_rows{b}", [8, P], F32R, attn) for b in range(2)]
        late = ExitStack()
        q_full = sb("q_full", [P, 2, HALF], F32, late)
        valT = sb("valT", [P, 2, HALF], F32, late)
        probs = [sb(f"probs{b}", [P, 2, HALF], F32, late) for b in range(4)]
        acc = [sb(f"acc{b}", [P, 2, HALF], F32, late) for b in range(2)]
        recip = sb("recip", [P, HALF], F32, late)
        oT = sb("oT", [P, HALF], F32, late)
        o_hi = sb("o_hi", [P, HALF], F32R, late)
        o_lo = sb("o_lo", [P, HALF], F32R, late)
        late.close()
        norm = ExitStack()
        x_in = sb("x_in", [P, ROWS // P, DM], F32, norm)
        norm.close()
        cen = [sb(f"cen{n}", [P, KD, HALF], F32, norm) for n in range(NBLK)]
        sq = [sb(f"sq{n}", [P, KD, HALF], F32, norm) for n in range(NBLK)]
        rstd = sb("rstd", [P, HALF], F32, norm)
        c_in = sb("c_in", [CROSS.ks, BATCH * CROSS.kt, DC], F32, norm)
        norm.close()
        attn.close()
        KF = DFF // P
        w1_raw = sb("w1_raw", [P, KD, 2 * DFF])
        w2_raw = sb("w2_raw", [P, KF, DM])
        w1_hi = sb("w1_hi", [P, KD, 2 * DFF], F32R)
        w1_lo = sb("w1_lo", [P, KD, 2 * DFF], F32R)
        w2_hi = sb("w2_hi", [P, KF, DM], F32R)
        w2_lo = sb("w2_lo", [P, KF, DM], F32R)
        gel = sb("gel", [P, 2, HALF])
        hid = sb("hid", [P, 2, HALF])
        hid_hi = sb("hid_hi", [P, 2, HALF], F32R)
        hid_lo = sb("hid_lo", [P, 2, HALF], F32R)
        yT = sb("yT", [P, KD, HALF])
        rows_out = sb("rows_out", [P, 4, DM])

        s_const = sem("const_set")
        s_identz = sem("ident_zeroed")
        s_klz = sem("kl_zeroed")
        s_pickz = sem("pick_zeroed")
        s_const_v = sem("const_set_dve")
        s_vec = sem("vectors_loaded")
        s_vec_turned = sem("vectors_turned")
        s_vecs = sem("vectors_ready")
        s_x = [sem(f"x_loaded{n}") for n in range(NBLK)]
        s_ctx = sem("context_loaded")
        s_xt_ready = sem("x_turned")
        s_xt = sem("x_copied")
        s_ct_ready = sem("context_turned")
        s_ct_hi = sem("context_hi")
        s_ct = sem("context_split")
        s_mean = sem("mean_ready")
        s_cen = sem("centred")
        s_sq = sem("squared")
        s_var = sem("variance_ready")
        s_std = sem("std_ready")
        s_rstd = sem("rstd_ready")
        s_spread = sem("rstd_spread")
        s_nrm = sem("normalised")
        s_aff = sem("affine_done")
        s_bias = sem("bias_added")
        s_hhi = sem("h_hi_ready")
        s_h = sem("h_ready")

        def names(pre):
            return {n: sem(f"{pre}_{n}") for n in (
                "w_loaded", "w_hi", "wq_lo", "w_lo", "wo_loaded", "wo_hi", "wo_lo", "prep_ready", "prep_free0", "prep_free1", "hi_ready",
                "k_twice", "q_lo", "q_again", "x_ready", "x_read", "m_cols", "m_moved0", "m_moved1", "s_ready", "exp_done", "pv_done", "acc_done",
                "sums_ready", "sums_read", "norm_done", "y_ready", "y_added", "o_hi", "o_lo")}

        sems = {SELF: names("self"), CROSS: names("cross")}
        s_w1 = [sem(f"ff_weights_loaded{i}") for i in range(3)]
        s_w1_hi = sem("ff_weights_hi")
        s_w1_lo = sem("ff_weights_split")
        s_gate = sem("gate_ready")
        s_lin = sem("linear_ready")
        s_gel = sem("gelu_done")
        s_hid = sem("hidden_done")
        s_hid_hi = sem("hidden_hi")
        s_hid_lo = sem("hidden_lo")
        s_y = sem("y_step")
        s_yT = sem("y_added")
        s_turn = sem("y_turned")
        s_rows = sem("rows_copied")
        s_out = sem("out_stored")

        W = {SELF: (io["sa_wq"], io["sa_wk"], io["sa_wv"], io["sa_wo"]),
             CROSS: (io["ca_wq"], io["ca_wk"], io["ca_wv"], io["ca_wo"])}
        SRC = {SELF: (h_hi, h_lo), CROSS: (c_hi, c_lo)}
        SC, PV, PREP, FOLD = 0, 2, 6, 7

        def prep_use(plan, kind, a, J, b):
            use = plan.at[kind] + a
            which = (plan.nprep * b + use) % plan.prep_banks
            g = plan.nprep * J + use
            return g, PREP - which, sems[plan][f"prep_free{which}"], g if plan.prep_banks == 1 else g // 2

        def cols(start, n):
            return bass.ds(start, n)

        block = ctx.enter_context(nc.Block())

        @block.sync
        def _(sp):
            def load_x(n):
                t = HALF // P
                sp.dma_start(x_in[:, n * t:(n + 1) * t, :],
                             io["x"].rearrange("b (t p) d -> p (b t) d", p=P)[:, n * t:(n + 1) * t, :]).then_inc(s_x[n], 16)

            load_x(0)
            load_x(1)
            for i, (g, b, nb) in enumerate((("ln1_g", "ln1_b", "sa_bo"), ("ln2_g", "ln2_b", "ca_bo"), ("ln3_g", "ln3_b", "ff_b2"))):
                for v, name in enumerate((g, b, nb)):
                    r = i * NORM_V + v * KD
                    sp.dma_start(vec_rows[r:r + KD, :], io[name].rearrange("(k p) -> k p", p=P)).then_inc(s_vec, 16)
            sp.dma_start(vec_rows[3 * NORM_V:, :], io["ff_b1"].rearrange("(k p) -> k p", p=P)).then_inc(s_vec, 16)
            load_x(2)
            load_x(3)
            sp.dma_start(c_in[:], io["ctx"].rearrange("b (t p) d -> p (b t) d", p=CROSS.ks)).then_inc(s_ctx, 16)

            def attention(plan, h_count):
                S = sems[plan]
                kk, kl = keys_hh[plan], keys_lm[plan]
                wq, wk, wv, wo = W[plan]

                def load_w(J):
                    p0 = fixed(sp, (J % PAIRS) * P)
                    after(sp, S["w_lo"], J)
                    for i, w in enumerate((wq, wk, wv)):
                        n, kin = (P, KD) if i == 0 else (plan.pin, plan.kin)
                        sp.dma_start(w_raw[0:n, i, 0:kin, :],
                                     w.rearrange("(k p) c -> p k c", p=n)[:, :, cols(p0, P)]).then_inc(S["w_loaded"], 16)

                def load_wo(J):
                    p0 = fixed(sp, (J % PAIRS) * P)
                    after(sp, S["wo_lo"], J)
                    sp.dma_start(wo_raw[:], wo[cols(p0, P), :]).then_inc(S["wo_loaded"], 16)

                def emit(steps, par):
                    for kind, J, a, dp in steps:
                        b = par ^ dp
                        if kind in plan.at:
                            g, prep, free, reads = prep_use(plan, kind, a, J, b)
                        if kind == "W":
                            load_w(J)
                        elif kind == "L":
                            load_wo(J)
                        elif kind == "M":
                            sp.wait_ge(free, reads + 1)
                            for h in range(2):
                                row = DH if h == 0 else 0
                                sp.dma_start(qm[b][row:row + 1, h, a * HALF:(a + 1) * HALF].rearrange("o (t c) -> o t c", t=4).bitcast(F32),
                                             m_rows[a][4 * h:4 * h + 4, :].bitcast(F32)).then_inc(S[f"m_moved{a}"], 16)

                if plan is CROSS:
                    sp.wait_ge(s_h, h_count)
                    for k in range(KD):
                        sp.dma_start(w1_raw[:, k, :], io["ff_w1"].rearrange("(k p) c -> p k c", p=P)[:, k, :]).then_inc(s_w1[k], 16)
                    sp.dma_start(w2_raw[:], io["ff_w2"].rearrange("(k p) c -> p k c", p=P)).then_inc(s_w1[2], 16)
                bodies("sp", sp, plan, emit)

            attention(SELF, NBLK)
            attention(CROSS, 2 * NBLK)
            out_v = out.rearrange("b (n t p) d -> p (b n) t d", p=P, t=4)
            with sp.Fori(0, NBLK) as n:
                for r in range(2):
                    sp.wait_ge(s_rows, 2 * n + r + 1)
                    sp.dma_start(out_v[:, cols(n, 1), 2 * r:2 * r + 2, :].rearrange("p o t d -> p (o t) d"),
                                 rows_out[:, 2 * r:2 * r + 2, :]).then_inc(s_out, 16)
            sp.wait_ge(s_out, 32 * NBLK)

        @block.tensor
        def _(pe):
            def bank(n, width=HALF):
                return psum[:, n, 0:width]

            def turn_in(n):
                pe.wait_ge(s_x[n], 16)
                for k in range(KD):
                    i = KD * n + k
                    after(pe, s_xt, i - 3)
                    for t in range(4):
                        mm = pe.transpose(psum[:, 4 + i % 4, t * P:(t + 1) * P], x_in[:, 4 * n + t, k * P:(k + 1) * P], ident[:])
                    mm.then_inc(s_xt_ready, 1)

            def turn_vectors():
                pe.wait_ge(s_vec, 16 * 10)
                pe.transpose(psum[:, 3, 0:3 * NORM_V + FF_V], vec_rows[:], ident[0:3 * NORM_V + FF_V, 0:3 * NORM_V + FF_V]).then_inc(s_vec_turned, 1)

            def turn_context():
                pe.wait_ge(s_xt, KD * NBLK)
                pe.wait_ge(s_ctx, 16)
                for k in range(KC):
                    for t in range(BATCH * CROSS.kt):
                        mm = pe.transpose(psum[0:PC, 6 + k, t * CROSS.ks:(t + 1) * CROSS.ks],
                                          c_in[:, t, k * PC:(k + 1) * PC], ident[0:CROSS.ks, 0:CROSS.ks])
                    mm.then_inc(s_ct_ready, 1)

            def mean(L, n):
                if L == 0:
                    pe.wait_ge(s_xt, KD * (n + 1))
                for k in range(KD):
                    mm = pe.matmul(bank(n), mean_w[:], xT[:, k, n * HALF:(n + 1) * HALF], start=(k == 0), stop=(k == KD - 1))
                mm.then_inc(s_mean, 1)

            def normalise(L):
                if L == 0:
                    pe.wait_ge(s_const, 1)
                    pe.wait_ge(s_const_v, 1)
                    turn_in(0)
                    turn_in(1)
                    mean(0, 0)
                    turn_vectors()
                    turn_in(2)
                    mean(0, 1)
                    turn_in(3)
                    mean(0, 2)
                    pe.wait_ge(s_vecs, 1)
                    mean(0, 3)
                    turn_context()
                else:
                    S = sems[SELF if L == 1 else CROSS]
                    pe.wait_ge(S["y_added"], 4 * NPAIR)
                    for n in range(NBLK):
                        mean(L, n)
                for n in range(NBLK):
                    pe.wait_ge(s_sq, NBLK * L + n + 1)
                    for k in range(KD):
                        mm = pe.matmul(psum[QUAD * n:QUAD * (n + 1), 5, :], mean_w[:, 0:QUAD], sq[n][:, k, :],
                                       start=(k == 0), stop=(k == KD - 1))
                mm.then_inc(s_var, 1)
                pe.wait_ge(s_rstd, L + 1)
                for n in range(NBLK):
                    pe.matmul(bank(n), pick[:, n, :], rstd[:], start=True, stop=True).then_inc(s_spread, 1)

            def attention(plan, h_count):
                S = sems[plan]
                kk, kl = keys_hh[plan], keys_lm[plan]
                src_hi, src_lo = SRC[plan]

                def project(which, src, kin, pin, c0, n, prep):
                    hi, lo = src
                    for k in range(kin):
                        a_hi, a_lo = w_hi[0:pin, which, k, :], w_lo[0:pin, which, k, :]
                        x_hi, x_lo = hi[0:pin, k, cols(c0, n)], lo[0:pin, k, cols(c0, n)]
                        for m, (w, x) in enumerate(((a_hi, x_hi), (a_hi, x_lo), (a_lo, x_hi))):
                            mm = pe.matmul(bank(prep, n), w, x, start=(k == 0 and m == 0), stop=(k == kin - 1 and m == 2))
                    return mm

                def emit(steps, par):
                    for kind, J, a, dp in steps:
                        b = par ^ dp
                        if kind in plan.at:
                            g, prep, free, reads = prep_use(plan, kind, a, J, b)
                        if kind in "KQV":
                            if kind == "K" and a == 0:
                                pe.wait_ge(S["w_lo"], J + 1)
                            after(pe, free, reads)
                            if kind == "Q":
                                mm = project(0, (h_hi, h_lo), KD, P, (J // PAIRS) * SEQ + a * HALF, HALF, prep)
                            else:
                                c0, n = plan.kcols[a]
                                mm = project(1 if kind == "K" else 2, (src_hi, src_lo), plan.kin, plan.pin,
                                             (J // PAIRS) * plan.keys + c0, n, prep)
                            mm.then_inc(S["prep_ready"], 1)
                        elif kind == "T":
                            _, _, projected, value_reads = prep_use(plan, "V", a, J, b)
                            pe.wait_ge(projected, value_reads + 1)
                            pe.wait_ge(free, reads)
                            n = plan.kt // plan.khalf
                            for t in range(n):
                                mm = pe.transpose(psum[0:plan.ks, prep, t * P:(t + 1) * P],
                                                  valT[:, a, t * plan.ks:(t + 1) * plan.ks], ident[:])
                            mm.then_inc(S["prep_ready"], 1)
                        elif kind == "X":
                            n = plan.tiles * J + a
                            if a == 0:
                                pe.wait_ge(S["k_twice"], plan.khalf * (J + 1))
                            if a in (0, plan.tiles // 2):
                                if plan is CROSS:
                                    pe.wait_ge(S["q_lo"], 4 * J + 2 + 2 * (a // (plan.tiles // 2)))
                                else:
                                    _, _, split, reads = prep_use(plan, "Q", a // (plan.tiles // 2), J, b)
                                    pe.wait_ge(split, reads + 1)
                            after(pe, S["x_read"], n - plan.mx_banks + 1)
                            if plan.khalf == 2:
                                half, h, t, kh = a // 16, a // 2 % 2, a // 4 % 4, a % 2
                                q0 = half * HALF + t * P
                                mm = pe.matmul(bank(PV + plan.pv_banks + a % plan.mx_banks), qq[b][:, h, q0:q0 + P], kk[b][:, h, kh * HALF:(kh + 1) * HALF],
                                               start=True, stop=True)
                            else:
                                for h in range(2):
                                    mm = pe.matmul(psum[:, PV + plan.pv_banks + a % plan.mx_banks, h * plan.keys:(h + 1) * plan.keys],
                                                   qq[b][:, h, a * P:(a + 1) * P], kk[b][:, h, 0:plan.keys], start=True, stop=True)
                            mm.then_inc(S["x_ready"], 1)
                        elif kind == "M":
                            pe.wait_ge(S["m_cols"], 2 * J + a + 1)
                            pe.wait_ge(free, reads)
                            pe.transpose(psum[:, prep, 0:P], m_cols[a][:], ident[:]).then_inc(S["prep_ready"], 1)
                        elif kind == "S":
                            u, h = a
                            half, kt = u // plan.kt, u % plan.kt
                            if kt == 0 and h == 0:
                                if half == 0:
                                    _, _, split, reads = prep_use(plan, "K", plan.khalf - 1, J, b)
                                    pe.wait_ge(split, reads + 1)
                                pe.wait_ge(S["q_again"], 2 * J + half + 1)
                                pe.wait_ge(S[f"m_moved{half}"], 32 * (J + 1))
                            ks = slice(kt * plan.ks, (kt + 1) * plan.ks)
                            qs = slice(half * HALF, (half + 1) * HALF)
                            after(pe, S["exp_done"], 2 * plan.units * J + 2 * u + h - 1)
                            pe.matmul(psum[0:plan.ks, SC + h, :], kk[b][:, h, ks], qq[b][:, h, qs], start=True, stop=False)
                            pe.matmul(psum[0:plan.ks, SC + h, :], kl[b][:, h, ks], qm[b][:, h, qs],
                                      start=False, stop=True).then_inc(S["s_ready"], 1)
                        elif kind == "P":
                            half, kt = a // plan.kt, a % plan.kt
                            if kt == 0:
                                after(pe, S["norm_done"], 2 * J + half + 1 - plan.pv_banks)
                                if half == 0:
                                    _, _, turned, reads = prep_use(plan, "T", plan.khalf - 1, J, b)
                                    pe.wait_ge(turned, reads + 1)
                            pe.wait_ge(S["exp_done"], 2 * plan.units * J + 2 * a + 2)
                            for h in range(2):
                                d = slice(h * DH, (h + 1) * DH)
                                mm = pe.matmul(psum[d, PV + half % plan.pv_banks, :], val[b][0:plan.ks, kt, d], probs[a % 4][0:plan.ks, h, :],
                                               start=(kt == 0), stop=(kt == plan.kt - 1))
                            mm.then_inc(S["pv_done"], 1)
                        elif kind == "D":
                            pe.wait_ge(S["acc_done"], (plan.kt - 1) * (2 * J + a + 1))
                            if a:
                                pe.wait_ge(S["sums_read"], 2 * J + 1)
                            after(pe, S["y_added"], 4 * J - 2 + 2 * a)
                            for h in range(2):
                                mm = pe.matmul(psum[h * DH:(h + 1) * DH, FOLD, :], ones[0:plan.ks, :], acc[a][0:plan.ks, h, :],
                                               start=True, stop=True)
                            mm.then_inc(S["sums_ready"], 1)
                        elif kind == "Y":
                            half, m = a
                            if m == 0:
                                pe.wait_ge(S["o_lo"], 2 * J + half + 1)
                                pe.wait_ge(S["wo_lo"], J + 1)
                            if m or (isinstance(J, int) and J == NPAIR - 1 and half == 1):
                                pe.wait_ge(S["y_added"], 4 * J + 2 * half + m)
                            else:
                                pe.wait_ge(S["sums_read"], 2 * J + 2 + half)
                            mc = slice(m * P, (m + 1) * P)
                            pe.matmul(bank(FOLD), wo_hi[b][:, mc], o_hi[:], start=True, stop=False)
                            pe.matmul(bank(FOLD), wo_hi[b][:, mc], o_lo[:], start=False, stop=False)
                            pe.matmul(bank(FOLD), wo_lo[b][:, mc], o_hi[:], start=False, stop=True).then_inc(S["y_ready"], 1)

                pe.wait_ge(s_h, h_count)
                pe.wait_ge(s_const_v, 3)
                if plan is CROSS:
                    pe.wait_ge(s_ct, KC)
                bodies("pe", pe, plan, emit)

            def feed_forward():
                def turn(n):
                    pe.wait_ge(s_yT, n + 1)
                    after(pe, s_rows, 2 * n)
                    for t in range(4):
                        for m in range(KD):
                            mm = pe.transpose(psum[:, 6 + t // 2, (t % 2) * DM + m * P:(t % 2) * DM + (m + 1) * P],
                                              yT[:, m, t * P:(t + 1) * P], ident[:])
                        if t % 2:
                            mm.then_inc(s_turn, 1)

                def down(n, f):
                    q = KF * n + f
                    if f == 0:
                        after(pe, s_yT, n)
                    if isinstance(n, int) and n == 0 and f == 0:
                        pe.wait_ge(s_w1_lo, KD + 1)
                    pe.wait_ge(s_hid_lo, q + 1)
                    for m in range(KD):
                        mc = slice(m * P, (m + 1) * P)
                        for i, (w, x) in enumerate(((w2_hi, hid_hi), (w2_hi, hid_lo), (w2_lo, hid_hi))):
                            mm = pe.matmul(bank(4 + m), w[:, f, mc], x[:, f % 2, :], start=(f == 0 and i == 0),
                                           stop=(f == KF - 1 and i == 2))
                    mm.then_inc(s_y, 1)

                def one(n, tail):
                    for f in range(KF):
                        q = KF * n + f
                        for c, bk, ready, read in ((DFF + f * P, 2 + f % 2, s_gate, s_gel), (f * P, f % 2, s_lin, s_hid)):
                            after(pe, read, q - 1)
                            for k in range(KD):
                                for i, (w, x) in enumerate(((w1_hi, h_hi), (w1_hi, h_lo), (w1_lo, h_hi))):
                                    mm = pe.matmul(bank(bk), w[:, k, c:c + P], x[:, k, cols(n * HALF, HALF)],
                                                   start=(k == 0 and i == 0), stop=(k == KD - 1 and i == 2))
                            mm.then_inc(ready, 1)
                        if f:
                            down(n, f - 1)
                        if f == 2 and tail:
                            turn(n - 1)
                    down(n, KF - 1)

                pe.wait_ge(s_w1_lo, KD)
                pe.wait_ge(s_h, 3 * NBLK)
                one(0, False)
                with pe.Fori(1, NBLK) as n:
                    one(n, True)
                turn(NBLK - 1)

            normalise(0)
            attention(SELF, NBLK)
            normalise(1)
            attention(CROSS, 2 * NBLK)
            normalise(2)
            feed_forward()

        @block.vector
        def _(dve):
            dve.memset(mean_w[:], 1.0 / DM)
            dve.memset(eps[:], EPS)
            dve.memset(pick[:], 0.0).then_inc(s_pickz, 1)
            dve.wait_ge(s_pickz, 1)
            for n in range(NBLK):
                dve.memset(pick[QUAD * n:QUAD * n + 1, n, :], 1.0)
            dve.memset(ones[:], 1.0).then_inc(s_const_v, 1)
            for b in range(2):
                dve.memset(m_cols[b][:], 0.0)
                dve.memset(qm[b][:].bitcast(F32), 0.0)
                for plan in (SELF, CROSS):
                    dve.memset(keys_lm[plan][b][:].bitcast(F32), 0.0).then_inc(s_klz, 1)
                dve.wait_ge(s_klz, 2 * (b + 1))
                for plan in (SELF, CROSS):
                    dve.memset(keys_lm[plan][b][DH:DH + 1, 0, :].bitcast(F32), -1.0)
                    last = dve.memset(keys_lm[plan][b][0:1, 1, :].bitcast(F32), -1.0)
                last.then_inc(s_const_v, 1)
            def copy_in(n):
                for k in range(KD):
                    i = KD * n + k
                    dve.wait_ge(s_xt_ready, i + 1)
                    dve.tensor_copy(xT[:, k, n * HALF:(n + 1) * HALF], psum[:, 4 + i % 4, :]).then_inc(s_xt, 1)

            def normalise(L):
                def centre(n):
                    dve.wait_ge(s_mean, NBLK * L + n + 1)
                    dve.tensor_tensor(cen[n][:], xT[:, :, n * HALF:(n + 1) * HALF], psum[:, n, :].unsqueeze(1).to_broadcast([P, KD, HALF]),
                                      ALU.subtract).then_inc(s_cen, 1)

                def scale(n):
                    dve.wait_ge(s_spread, NBLK * L + n + 1)
                    dve.tensor_tensor(cen[n][:], cen[n][:], psum[:, n, :].unsqueeze(1).to_broadcast([P, KD, HALF]), ALU.mult).then_inc(s_nrm, 1)

                def low(n):
                    dve.wait_ge(s_hhi, NBLK * L + n + 1)
                    dve.tensor_tensor(h_lo[:, :, n * HALF:(n + 1) * HALF], sq[n][:], h_hi[:, :, n * HALF:(n + 1) * HALF],
                                      ALU.subtract).then_inc(s_h, 1)

                if L == 0:
                    copy_in(0)
                    copy_in(1)
                    dve.wait_ge(s_vec_turned, 1)
                    dve.tensor_copy(vecs[:], psum[:, 3, 0:3 * NORM_V + FF_V]).then_inc(s_vecs, 1)
                    centre(0)
                    copy_in(2)
                    centre(1)
                    copy_in(3)
                    centre(2)
                    centre(3)
                    for k in range(KC):
                        dve.wait_ge(s_ct_hi, k + 1)
                        dve.tensor_tensor(c_lo[:, k, :], psum[0:PC, 6 + k, 0:BATCH * TC], c_hi[:, k, :], ALU.subtract).then_inc(s_ct, 1)
                else:
                    for n in range(NBLK):
                        centre(n)
                dve.wait_ge(s_std, L + 1)
                dve.reciprocal(rstd[:], rstd[:]).then_inc(s_rstd, 1)
                for n in range(NBLK):
                    scale(n)
                    if n >= 2:
                        low(n - 2)
                low(NBLK - 2)
                low(NBLK - 1)

            def attention(plan, h_count):
                S = sems[plan]
                kk, kl = keys_hh[plan], keys_lm[plan]

                def emit(steps, par):
                    for kind, J, a, dp in steps:
                        b = par ^ dp
                        if kind in plan.at:
                            g, prep, free, reads = prep_use(plan, kind, a, J, b)
                        if kind == "K" or (kind == "Q" and plan is SELF):
                            c0, n = plan.kcols[a] if kind == "K" else (a * HALF, HALF)
                            hi, lo = (kk[b], kl[b]) if kind == "K" else (qq[b], qq[b])
                            dve.wait_ge(S["hi_ready"], plan.nsplit * J + plan.at[kind] + a + 1)
                            for h in range(2):
                                own = slice(h * DH, (h + 1) * DH)
                                to = own if kind == "K" else slice((1 - h) * DH, (2 - h) * DH)
                                op = dve.tensor_tensor(lo[to, h, c0:c0 + n], psum[own, prep, 0:n], hi[own, h, c0:c0 + n], ALU.subtract)
                            op.then_inc(free, 1)
                        elif kind == "X":
                            dve.wait_ge(S["x_ready"], plan.tiles * J + a + 1)
                            if plan.khalf == 2:
                                half, h, t, kh = a // 16, a // 2 % 2, a // 4 % 4, a % 2
                                dve.tensor_reduce(m_part[:, half, h, t, kh:kh + 1], psum[:, PV + plan.pv_banks + a % plan.mx_banks, :], AX.X,
                                                  ALU.max).then_inc(S["x_read"], 1)
                            else:
                                dve.tensor_reduce(m_part[:, a // 4, :, a % 4, 0],
                                                  psum[:, PV + plan.pv_banks + a % plan.mx_banks, 0:2 * plan.keys].rearrange("p (h k) -> p h k", h=2),
                                                  AX.X, ALU.max).then_inc(S["x_read"], 1)
                        elif kind == "C":
                            dve.wait_ge(S["x_read"], plan.tiles * J + plan.tiles // 2 * (a + 1))
                            dve.tensor_reduce(m_cols[a][:, 0:8], m_part[:, a, :, :, 0:plan.khalf].rearrange("p h t k -> p (h t) k"),
                                              AX.X, ALU.max).then_inc(S["m_cols"], 1)
                        elif kind == "M":
                            after(dve, S[f"m_moved{a}"], 32 * J)
                            dve.wait_ge(S["prep_ready"], g + 1)
                            dve.tensor_copy(m_rows[a][:], psum[0:8, prep, 0:P]).then_inc(free, 1)
                        elif kind == "D":
                            dve.wait_ge(S["sums_ready"], 2 * J + a + 1)
                            after(dve, S["norm_done"], 2 * J + a)
                            dve.reciprocal(recip[:], psum[:, FOLD, :]).then_inc(S["sums_read"], 1)
                        elif kind == "R":
                            dve.wait_ge(S["sums_read"], 2 * J + a + 1)
                            dve.wait_ge(S["pv_done"], plan.units * J + plan.kt * (a + 1))
                            after(dve, S["o_lo"], 2 * J + a)
                            dve.tensor_tensor(oT[:], psum[:, PV + a % plan.pv_banks, :], recip[:], ALU.mult).then_inc(S["norm_done"], 1)
                        elif kind == "Y":
                            half, m = a
                            dve.wait_ge(S["y_ready"], 4 * J + 2 * half + m + 1)
                            x = xT[:, m, cols((J // PAIRS) * SEQ + half * HALF, HALF)]
                            dve.tensor_tensor(x, x, psum[:, FOLD, :], ALU.add).then_inc(S["y_added"], 1)

                dve.wait_ge(s_h, h_count)
                dve.wait_ge(s_bias, h_count)
                bodies("dve", dve, plan, emit)

            def feed_forward():
                dve.wait_ge(s_bias, 3 * NBLK)

                def lo(n, f):
                    q = KF * n + f
                    dve.wait_ge(s_hid_hi, q + 1)
                    dve.tensor_tensor(hid_lo[:, f % 2, :], hid[:, f % 2, :], hid_hi[:, f % 2, :], ALU.subtract).then_inc(s_hid_lo, 1)

                def one(n):
                    for f in range(KF):
                        q = KF * n + f
                        dve.wait_ge(s_gel, q + 1)
                        dve.wait_ge(s_lin, q + 1)
                        if f >= 2 or not isinstance(n, int):
                            after(dve, s_hid_lo, q - 1)
                        dve.scalar_tensor_tensor(hid[:, f % 2, :], psum[:, f % 2, :], ff_b1(f), gel[:, f % 2, :],
                                                 ALU.add, ALU.mult).then_inc(s_hid, 1)
                        lo(n, f)
                    dve.wait_ge(s_y, KF * (n + 1))
                    after(dve, s_turn, 2 * n)
                    dve.tensor_tensor(yT[:], psum[:, 4:6, :], xT[:, :, cols(n * HALF, HALF)], ALU.add).then_inc(s_yT, 1)

                one(0)
                with dve.Fori(1, NBLK) as n:
                    one(n)

            normalise(0)
            attention(SELF, NBLK)
            normalise(1)
            attention(CROSS, 2 * NBLK)
            normalise(2)
            feed_forward()

        @block.scalar
        def _(act):
            def normalise(L):
                if L == 0:
                    act.wait_ge(s_const_v, 1)
                for n in range(NBLK):
                    act.wait_ge(s_cen, NBLK * L + n + 1)
                    act.activation(sq[n][:], cen[n][:], ACT.Square).then_inc(s_sq, 1)
                if L == 0:
                    for k in range(KC):
                        act.wait_ge(s_ct_ready, k + 1)
                        act.activation(c_hi[:, k, :], psum[0:PC, 6 + k, 0:BATCH * TC], ACT.Copy).then_inc(s_ct_hi, 1)
                act.wait_ge(s_var, L + 1)
                act.activation(rstd[:], psum[:, 5, :], ACT.Sqrt, bias=eps[:]).then_inc(s_std, 1)
                if L == 0:
                    act.wait_ge(s_vecs, 1)
                for n in range(NBLK):
                    act.wait_ge(s_nrm, NBLK * L + n + 1)
                    for k in range(KD):
                        op = act.activation(sq[n][:, k, :], cen[n][:, k, :], ACT.Identity, scale=ln_g(L, k), bias=ln_b(L, k))
                    op.then_inc(s_aff, 1)
                    act.wait_ge(s_aff, NBLK * L + n + 1)
                    act.activation(h_hi[:, :, n * HALF:(n + 1) * HALF], sq[n][:], ACT.Copy).then_inc(s_hhi, 1)

            def attention(plan, h_count):
                S = sems[plan]
                kk, kl = keys_hh[plan], keys_lm[plan]

                def split_w(J):
                    act.wait_ge(S["w_loaded"], 48 * (J + 1))
                    after(act, S["prep_ready"], plan.nprep * (J - 1) + plan.at["T"])
                    if plan is SELF:
                        act.activation(w_hi[:], w_raw[:], ACT.Copy).then_inc(S["w_hi"], 1)
                    else:
                        act.activation(w_hi[:, 0, :, :], w_raw[:, 0, :, :], ACT.Copy).then_inc(S["w_hi"], 1)
                        act.activation(w_hi[0:PC, 1:3, :, :], w_raw[0:PC, 1:3, :, :], ACT.Copy).then_inc(S["w_hi"], 1)

                def emit(steps, par):
                    for kind, J, a, dp in steps:
                        b = par ^ dp
                        if kind in plan.at:
                            g, prep, free, reads = prep_use(plan, kind, a, J, b)
                        if kind == "W":
                            split_w(J)
                        elif kind == "O":
                            act.wait_ge(S["wo_loaded"], 16 * (J + 1))
                            after(act, S["y_ready"], 4 * (J - 1))
                            act.activation(wo_hi[b][:], wo_raw[:], ACT.Copy).then_inc(S["wo_hi"], 1)
                        elif kind == "K":
                            c0, n = plan.kcols[a]
                            act.wait_ge(S["prep_ready"], g + 1)
                            if a == 0:
                                after(act, S["s_ready"], 2 * plan.units * (J - 1))
                            for h in range(2):
                                own = slice(h * DH, (h + 1) * DH)
                                op = act.activation(kk[b][own, h, c0:c0 + n], psum[own, prep, 0:n], ACT.Copy)
                            op.then_inc(S["hi_ready"], 1)
                            act.wait_ge(S["hi_ready"], plan.nsplit * J + a + 1)
                            for h in range(2):
                                own, other = slice(h * DH, (h + 1) * DH), slice((1 - h) * DH, (2 - h) * DH)
                                op = act.activation(kk[b][other, h, c0:c0 + n], kk[b][own, h, c0:c0 + n], ACT.Copy)
                            op.then_inc(S["k_twice"], 1)
                        elif kind == "Q":
                            act.wait_ge(S["prep_ready"], g + 1)
                            for h in range(2):
                                own = slice(h * DH, (h + 1) * DH)
                                op = act.activation(qq[b][own, h, a * HALF:(a + 1) * HALF], psum[own, prep, :], ACT.Copy)
                            op.then_inc(S["hi_ready"], 1)
                            if plan is CROSS:
                                after(act, S["q_lo"], 4 * J + 2 * a - 2)
                                act.activation(q_full[:, a, :], psum[:, prep, :], ACT.Copy).then_inc(free, 1)
                        elif kind == "B":
                            act.wait_ge(S["hi_ready"], plan.nsplit * J + plan.khalf + a + 1)
                            for h in range(2):
                                own, half = slice(h * DH, (h + 1) * DH), slice(a * HALF, (a + 1) * HALF)
                                op = act.activation(qm[b][own, h, half], qq[b][own, h, half], ACT.Copy)
                            op.then_inc(S["q_again"], 1)
                        elif kind == "V":
                            act.wait_ge(S["prep_ready"], g + 1)
                            n = plan.kcols[a][1]
                            act.activation(valT[:, a, 0:n], psum[:, prep, 0:n], ACT.Copy).then_inc(free, 1)
                        elif kind == "T":
                            act.wait_ge(S["prep_ready"], g + 1)
                            after(act, S["pv_done"], plan.units * (J - 1))
                            n = plan.kt // plan.khalf
                            act.activation(val[b][0:plan.ks, a * n:(a + 1) * n, :],
                                           psum[0:plan.ks, prep, 0:n * P].rearrange("p (t d) -> p t d", t=n),
                                           ACT.Copy).then_inc(free, 1)
                        elif kind == "S":
                            u, h = a
                            if h == 0:
                                after(act, S["pv_done"], plan.units * J + u - 3)
                                pair, back = (J, u - 4) if u >= 4 else (J - 1, u - 4 + plan.units)
                                after(act, S["acc_done"], 2 * (plan.kt - 1) * pair + plan.added(back))
                            act.wait_ge(S["s_ready"], 2 * plan.units * J + 2 * u + h + 1)
                            act.activation(probs[u % 4][0:plan.ks, h, :], psum[0:plan.ks, SC + h, :], ACT.Exp,
                                           scale=SCALE).then_inc(S["exp_done"], 1)
                        elif kind == "N":
                            act.wait_ge(S["norm_done"], 2 * J + a + 1)
                            after(act, S["y_ready"], 4 * J + 2 * a)
                            act.activation(o_hi[:], oT[:], ACT.Copy).then_inc(S["o_hi"], 1)

                bodies("act", act, plan, emit)

            def feed_forward():
                act.wait_ge(s_vecs, 1)

                def hi(n, f):
                    q = KF * n + f
                    act.wait_ge(s_hid, q + 1)
                    after(act, s_y, q - 1)
                    act.activation(hid_hi[:, f % 2, :], hid[:, f % 2, :], ACT.Copy).then_inc(s_hid_hi, 1)

                def store(n):
                    for r in range(2):
                        act.wait_ge(s_turn, 2 * n + r + 1)
                        after(act, s_out, 32 * n)
                        act.activation(rows_out[:, 2 * r:2 * r + 2, :],
                                       psum[:, 6 + r, :].rearrange("p (t d) -> p t d", t=2), ACT.Copy).then_inc(s_rows, 1)

                def one(n, tail):
                    for f in range(KF):
                        q = KF * n + f
                        if f:
                            hi(n, f - 1)
                        act.wait_ge(s_gate, q + 1)
                        after(act, s_hid, q - 1)
                        act.activation(gel[:, f % 2, :], psum[:, 2 + f % 2, :], ACT.Gelu,
                                       bias=ff_b1(KF + f)).then_inc(s_gel, 1)
                        if f == 3 and tail:
                            store(n - 1)
                    hi(n, KF - 1)

                one(0, False)
                with act.Fori(1, NBLK) as n:
                    one(n, True)
                store(NBLK - 1)

            normalise(0)
            attention(SELF, NBLK)
            normalise(1)
            attention(CROSS, 2 * NBLK)
            act.wait_ge(sems[CROSS]["y_added"], 4 * NPAIR)
            act.wait_ge(sems[CROSS]["w_lo"], NPAIR)
            for k in range(KD):
                act.wait_ge(s_w1[k], 16)
                act.activation(w1_hi[:, k, :], w1_raw[:, k, :], ACT.Copy).then_inc(s_w1_hi, 1)
            act.wait_ge(s_w1[2], 16)
            act.activation(w2_hi[:], w2_raw[:], ACT.Copy).then_inc(s_w1_hi, 1)
            normalise(2)
            feed_forward()

        @block.gpsimd
        def _(pool):
            pool.memset(ident[:], 0.0).then_inc(s_identz, 1)
            pool.wait_ge(s_identz, 1)
            pool.affine_select(out=ident[:], in_=ident[:], compare_op=ALU.not_equal, fill=1.0, base=0,
                               pattern=[[-1, P]], channel_multiplier=1).then_inc(s_const, 1)
            def attention(plan, h_count):
                S = sems[plan]
                kk, kl = keys_hh[plan], keys_lm[plan]

                def split_w(J):
                    if plan is SELF:
                        pool.wait_ge(S["w_hi"], J + 1)
                        pool.tensor_tensor(w_lo[:], w_raw[:], w_hi[:], ALU.subtract).then_inc(S["w_lo"], 1)
                    else:
                        pool.wait_ge(S["w_hi"], 2 * J + 2)
                        pool.tensor_tensor(w_lo[:, 0, :, :], w_raw[:, 0, :, :], w_hi[:, 0, :, :], ALU.subtract).then_inc(S["wq_lo"], 1)
                        pool.wait_ge(S["wq_lo"], J + 1)
                        pool.tensor_tensor(w_lo[0:PC, 1:3, :, :], w_raw[0:PC, 1:3, :, :], w_hi[0:PC, 1:3, :, :],
                                           ALU.subtract).then_inc(S["w_lo"], 1)
                        pool.wait_ge(S["w_lo"], J + 1)

                def emit(steps, par):
                    for kind, J, a, dp in steps:
                        b = par ^ dp
                        if kind in plan.at:
                            g, prep, free, reads = prep_use(plan, kind, a, J, b)
                        if kind == "W":
                            split_w(J)
                        elif kind == "O":
                            pool.wait_ge(S["wo_hi"], J + 1)
                            pool.tensor_tensor(wo_lo[b][:], wo_raw[:], wo_hi[b][:], ALU.subtract).then_inc(S["wo_lo"], 1)
                            if plan is CROSS:
                                pool.wait_ge(S["wo_lo"], J + 1)
                        elif kind == "S":
                            u, h = a
                            half, kt = u // plan.kt, u % plan.kt
                            if kt == 0 or h == 0:
                                continue
                            now, last = probs[u % 4][0:plan.ks], probs[(u - 1) % 4][0:plan.ks]
                            total = acc[half][0:plan.ks]
                            summed = 2 * (plan.kt - 1) * J + plan.added(u)
                            if kt == 1:
                                after(pool, S["sums_ready"], 2 * (J - 1) + half + 1)
                            else:
                                pool.wait_ge(S["acc_done"], summed - 1)
                            pool.wait_ge(S["exp_done"], 2 * plan.units * J + 2 * u + 2)
                            pool.tensor_tensor(total, last if kt == 1 else total, now, ALU.add).then_inc(S["acc_done"], 1)
                            if plan is CROSS:
                                pool.wait_ge(S["acc_done"], summed)
                        elif kind == "Q" and plan is CROSS:
                            pool.wait_ge(S["hi_ready"], plan.nsplit * J + plan.khalf + a + 1)
                            pool.wait_ge(free, reads + 1)
                            for h in range(2):
                                own, other = slice(h * DH, (h + 1) * DH), slice((1 - h) * DH, (2 - h) * DH)
                                half = slice(a * HALF, (a + 1) * HALF)
                                pool.tensor_tensor(qq[b][other, h, half], q_full[own, a, :], qq[b][own, h, half],
                                                   ALU.subtract).then_inc(S["q_lo"], 1)
                                pool.wait_ge(S["q_lo"], 4 * J + 2 * a + h + 1)
                        elif kind == "N":
                            pool.wait_ge(S["o_hi"], 2 * J + a + 1)
                            pool.tensor_tensor(o_lo[:], oT[:], o_hi[:], ALU.subtract).then_inc(S["o_lo"], 1)
                            if plan is CROSS:
                                pool.wait_ge(S["o_lo"], 2 * J + a + 1)

                bodies("pool", pool, plan, emit)

            def normalise(L):
                def add_bias(n):
                    pool.wait_ge(s_cen, NBLK * L + n + 1)
                    for k in range(KD):
                        op = pool.tensor_scalar(xT[:, k, n * HALF:(n + 1) * HALF], xT[:, k, n * HALF:(n + 1) * HALF], out_b(L, k), None, ALU.add)
                    op.then_inc(s_bias, 1)

                if L == 0:
                    pool.wait_ge(s_vecs, 1)
                for n in range(NBLK):
                    add_bias(n)

            def split_ff(i, raw, hi, lo):
                pool.wait_ge(s_w1_hi, i + 1)
                pool.tensor_tensor(lo, raw, hi, ALU.subtract).then_inc(s_w1_lo, 1)

            normalise(0)
            attention(SELF, NBLK)
            normalise(1)
            attention(CROSS, 2 * NBLK)
            split_ff(0, w1_raw[:, 0, :], w1_hi[:, 0, :], w1_lo[:, 0, :])
            split_ff(1, w1_raw[:, 1, :], w1_hi[:, 1, :], w1_lo[:, 1, :])
            split_ff(2, w2_raw[:], w2_hi[:], w2_lo[:])
            normalise(2)


_NAMES = {"x": "x", "ctx_768": "ctx"}
_PREFIX = "L0_xattn_"
_INS = ["x", "ctx_768"] + [_PREFIX + n for n in (
    "ln1_g", "ln1_b", "ln2_g", "ln2_b", "ln3_g", "ln3_b", "sa_wq", "sa_wk", "sa_wv", "sa_wo", "sa_bo",
    "ca_wq", "ca_wk", "ca_wv", "ca_wo", "ca_bo", "ff_w1", "ff_b1", "ff_w2", "ff_b2")]


def kernel(**inputs):
    import numpy as _np
    import concourse.bacc as _bacc
    from concourse import mybir as _mybir
    from concourse.bass_utils import run_bass_kernel_spmd as _run

    nc = _bacc.Bacc("TRN2", target_bir_lowering=False, num_devices=1)
    arrays, io = {}, {}
    for name in _INS:
        a = _np.ascontiguousarray(inputs[name])
        arrays[f"in_{name}"] = a
        io[_NAMES.get(name, name.removeprefix(_PREFIX))] = nc.dram_tensor(
            f"in_{name}", a.shape, _mybir.dt.from_np(a.dtype), kind="ExternalInput").ap()
    out = nc.dram_tensor("out", (BATCH, SEQ, DM), _mybir.dt.float32, kind="ExternalOutput").ap()
    block_kernel(nc, io, out)
    r = _run(nc, [arrays], core_ids=[0])
    return r.results[0]["out"]
```

```python
from contextlib import ExitStack

import concourse.bass as bass
from concourse import mybir

F32 = mybir.dt.float32
F32R = mybir.dt.float32r
ALU = mybir.AluOpType
ACT = mybir.ActivationFunctionType
AX = mybir.AxisListType

BATCH, SEQ, DM = 2, 1024, 256
DC, TC = 192, 154
HEADS, DH = 16, 64
DA = HEADS * DH
DFF = 1024
ROWS = BATCH * SEQ
P = 128
KD = DM // P
KC, PC = 2, DC // 2
HALF = 512
NBLK = ROWS // HALF
VROWS = P // 2
PAIRS = HEADS // 2
NPAIR = BATCH * PAIRS
EPS = 1e-5
SCALE = DH ** -0.5


SELF_ORDER = {
    "sp": "L- M1- M0 W++",
    "pe": "S0.0 S0.1 K0+ P13- S1.0 P14- S1.1 D1- K1+ S2.0 S2.1 P15- P0 P1 S3.0 Q0+ S3.1 S4.0 P2 S4.1 S5.0 "
          "X0+ Q1+ X1+ S5.1 X2+ S6.0 Y0.0- X3+ P3 X4+ V0+ X5+ X6+ P4 V1+ X7+ X8+ P5 X9+ S6.1 X10+ S7.0 "
          "X11+ P6 X12+ T0+ X13+ S7.1 X14+ S8.0 Y0.1- S8.1 X15+ X16+ P7 X17+ S9.0 X18+ T1+ X19+ S9.1 X20+ "
          "S10.0 X21+ S10.1 X22+ S11.0 X23+ P8 X24+ X25+ P9 X26+ S11.1 X27+ S12.0 X28+ M0+ S12.1 D0 S13.0 "
          "S13.1 P10 X29+ P11 S14.0 X30+ S14.1 Y1.0- X31+ P12 S15.0 S15.1 Y1.1- M1+",
    "dve": "R0- K0+ D1- K1+ Q0+ X0+ X1+ X2+ Q1+ X3+ X4+ X5+ X6+ X7+ X8+ X9+ X10+ Y0.0- X11+ X12+ X13+ R1- "
           "X14+ Y0.1- X15+ X16+ C0+ X17+ X18+ X19+ X20+ X21+ X22+ X23+ X24+ X25+ X26+ X27+ X28+ M0+ D0 "
           "X29+ X30+ Y1.0- X31+ C1+ M1+ Y1.1-",
    "act": "S0.0 S0.1 K0+ N0- S1.0 S1.1 K1+ S2.0 S2.1 S3.0 Q0+ S3.1 S4.0 S4.1 S5.0 Q1+ V0+ S5.1 V1+ S6.0 "
           "B0+ S6.1 S7.0 B1+ T0+ S7.1 S8.0 N1- W++ S8.1 S9.0 S9.1 S10.0 S10.1 S11.0 T1+ S11.1 S12.0 S12.1 "
           "S13.0 S13.1 S14.0 S14.1 S15.0 S15.1 O+",
    "pool": "W++ O S10.1 S11.1 S12.1 S13.1 S14.1 S15.1 S1.1+ S2.1+ S3.1+ N0 S4.1+ S5.1+ S6.1+ S7.1+ N1 S9.1+",
}
CROSS_ORDER = {
    "sp": "L W++ M0+ M1+",
    "pe": "M1 K+ Q0+ D1- Q1+ S0.1 S1.0 S1.1 V+ X0+ Y0.0- X1+ S2.0 X2+ S2.1 T+ X3+ Y0.1- X4+ P0 M0+ X5+ D0 "
          "S3.0 P1 S3.1 P2 X6+ S0.0+ Y1.0- X7+ P3 Y1.1-",
    "dve": "K+ D1- X0+ R1- X1+ Y0.0- X2+ X3+ C0+ Y0.1- X4+ M0+ X5+ D0 X6+ Y1.0- X7+ C1+ R0 M1+ Y1.1-",
    "act": "S3.1- T N0- K+ Q0+ S0.0 S0.1 Q1+ S1.0 B0+ S1.1 V+ W++ S2.0 N1- S2.1 B1+ O S3.0",
    "pool": "S3.1- N0- Q0+ Q1+ S1.1 W++ N1- O",
}


def read_order(text):
    which = {"-": "prev", "": "cur", "+": "next", "++": "after"}
    out = []
    for word in text.split():
        name = word.rstrip("+-")
        args = tuple(int(n) for n in name[1:].split(".")) if name[1:] else (0,)
        out.append((name[0], which[word[len(name):]], args if len(args) == 2 else args[0]))
    return out


class Plan:

    def __init__(self, own):
        self.own = own
        self.keys = SEQ if own else TC
        self.ks = P if own else TC // 2
        self.kt = self.keys // self.ks
        self.units = 2 * self.kt
        self.kin = KD if own else KC
        self.pin = P if own else PC
        self.kcols = [(c, min(HALF, self.keys - c)) for c in range(0, self.keys, HALF)]
        self.khalf = len(self.kcols)
        self.prep = (["K"] * self.khalf + ["Q"] * 2 + ["V"] * self.khalf + ["T"] * self.khalf + ["M"] * 2)
        self.nprep = len(self.prep)
        self.nsplit = self.khalf + 2
        self.at = {"K": 0, "Q": self.khalf, "V": self.khalf + 2, "T": 2 * self.khalf + 2, "M": 3 * self.khalf + 2}
        self.tiles = 16 * self.khalf if own else 8
        self.pv_banks, self.mx_banks, self.prep_banks = (2, 2, 1) if own else (2, 1, 2)
        self.steps = {e: read_order(text) for e, text in (SELF_ORDER if own else CROSS_ORDER).items()}

    def order(self, engine, j, have):
        of = {"prev": j - 1, "cur": j, "next": j + 1, "after": j + 2}
        par = {"prev": 1, "cur": 0, "next": 1, "after": 0}
        return [(kind, of[w], a, par[w]) for kind, w, a in self.steps[engine] if w in have]

    def added(self, u):
        return (u // self.kt) * (self.kt - 1) + max(u % self.kt, 1)


SELF, CROSS = Plan(True), Plan(False)


def after(eng, sem, value):
    if not isinstance(value, int) or value > 0:
        eng.wait_ge(sem, value)


def fixed(eng, value):
    return value if isinstance(value, int) else eng.snap(value)


def bodies(engine, eng, plan, emit, between=None, ending=None):
    emit(plan.order(engine, -2, ("after",)), 0)
    if between:
        between()
    emit(plan.order(engine, -1, ("next", "after")), 1)
    emit(plan.order(engine, 0, ("cur", "next", "after")), 0)
    emit(plan.order(engine, 1, ("prev", "cur", "next", "after")), 1)
    with eng.Fori(2, NPAIR - 3, 2) as j:
        emit(plan.order(engine, j, ("prev", "cur", "next", "after")), 0)
        emit(plan.order(engine, j + 1, ("prev", "cur", "next", "after")), 1)
    emit(plan.order(engine, NPAIR - 2, ("prev", "cur", "next")), 0)
    emit(plan.order(engine, NPAIR - 1, ("prev", "cur")), 1)
    if ending:
        ending()
    emit(plan.order(engine, NPAIR, ("prev",)), 0)


def block_kernel(nc, io, out):
    with ExitStack() as ctx:
        def sem(name):
            return ctx.enter_context(nc.semaphore(name))

        def sb(name, shape, dt=F32, of=ctx):
            return of.enter_context(nc.sbuf_tensor(name, shape, dt))

        xT = sb("xT", [P, KD, ROWS])
        h_hi = sb("h_hi", [P, KD, ROWS], F32R)
        h_lo = sb("h_lo", [P, KD, ROWS], F32R)
        ident = sb("ident", [P, P])
        ones = sb("ones", [P, DH])
        mean_w = sb("mean_w", [P, P])
        eps = sb("eps", [P, 1])
        pick = sb("pick", [P, 2, P])
        NORM_V, FF_V = 3 * KD, 2 * DFF // P
        vecs = sb("vecs", [P, 3 * NORM_V + FF_V])
        vec_rows = sb("vec_rows", [3 * NORM_V + FF_V, P])
        ln_g = lambda L, k: vecs[:, L * NORM_V + k:L * NORM_V + k + 1]
        ln_b = lambda L, k: vecs[:, L * NORM_V + KD + k:L * NORM_V + KD + k + 1]
        out_b = lambda L, k: vecs[:, L * NORM_V + 2 * KD + k:L * NORM_V + 2 * KD + k + 1]
        ff_b1 = lambda f: vecs[:, 3 * NORM_V + f:3 * NORM_V + f + 1]
        psum = ctx.enter_context(nc.psum_tensor("psum", [P, 8, HALF], F32))

        attn = ExitStack()
        keys_hh, keys_lm = {}, {}
        for plan, of in ((SELF, "self"), (CROSS, "cross")):
            keys_hh[plan] = [sb(f"{of}_keys_hh{b}", [P, 2, plan.keys], F32R, attn) for b in range(2)]
            keys_lm[plan] = [sb(f"{of}_keys_lm{b}", [P, 2, plan.keys], F32R, attn) for b in range(2)]
        c_hi = sb("c_hi", [PC, KC, BATCH * TC], F32R, attn)
        c_lo = sb("c_lo", [PC, KC, BATCH * TC], F32R, attn)
        w_raw = sb("w_raw", [P, 3, KD, P], F32, attn)
        w_hi = sb("w_hi", [P, 3, KD, P], F32R, attn)
        w_lo = sb("w_lo", [P, 3, KD, P], F32R, attn)
        wo_raw = sb("wo_raw", [P, DM], F32, attn)
        wo_hi = [sb(f"wo_hi{b}", [P, DM], F32R, attn) for b in range(2)]
        wo_lo = [sb(f"wo_lo{b}", [P, DM], F32R, attn) for b in range(2)]
        qq = [sb(f"qq{b}", [P, 2, SEQ], F32R, attn) for b in range(2)]
        qm = [sb(f"qm{b}", [P, 2, SEQ], F32R, attn) for b in range(2)]
        val = [sb(f"val{b}", [P, SELF.kt, P], F32, attn) for b in range(2)]
        m_part = sb("m_part", [P, 2, 2, 4, 2], F32, attn)
        m_cols = [sb(f"m_cols{b}", [P, P], F32, attn) for b in range(2)]
        m_rows = [sb(f"m_rows{b}", [8, P], F32R, attn) for b in range(2)]
        late = ExitStack()
        q_full = sb("q_full", [P, 2, HALF], F32, late)
        valT = sb("valT", [P, 2, HALF], F32, late)
        probs = [sb(f"probs{b}", [P, 2, HALF], F32, late) for b in range(4)]
        acc = [sb(f"acc{b}", [P, 2, HALF], F32, late) for b in range(2)]
        recip = sb("recip", [P, HALF], F32, late)
        oT = sb("oT", [P, HALF], F32, late)
        o_hi = sb("o_hi", [P, HALF], F32R, late)
        o_lo = sb("o_lo", [P, HALF], F32R, late)
        late.close()
        norm = ExitStack()
        x_in = sb("x_in", [P, ROWS // P, DM], F32, norm)
        norm.close()
        cen = [sb(f"cen{n}", [P, KD, HALF], F32, norm) for n in range(NBLK)]
        sq = [sb(f"sq{n}", [P, KD, HALF], F32, norm) for n in range(NBLK)]
        rstd = sb("rstd", [P, HALF], F32, norm)
        c_in = sb("c_in", [CROSS.ks, BATCH * CROSS.kt, DC], F32, norm)
        rstd_second = sb("rstd_second", [P, HALF], F32, norm)
        norm.close()
        attn.close()

        class Part:

            def __init__(self, L, second):
                self.L = L
                self.blocks = [2, 3] if second else [0, 1]
                self.number = 2 * L + second
                self.var_bank = ((5, 4) if L == 0 else (1, 0))[second]
                first = ((0, 2), (4, 2), (4, 6))[L][second]
                self.mean_bank = {n: first + n % 2 for n in self.blocks}
                self.rstd = rstd_second if second else rstd

        def parts(L):
            return [Part(L, 0), Part(L, 1)]

        KF = DFF // P
        w1_raw = sb("w1_raw", [P, KD, 2 * DFF])
        w2_raw = sb("w2_raw", [P, KF, DM])
        w1_hi = sb("w1_hi", [P, KD, 2 * DFF], F32R)
        w1_lo = sb("w1_lo", [P, KD, 2 * DFF], F32R)
        w2_hi = sb("w2_hi", [P, KF, DM], F32R)
        w2_lo = sb("w2_lo", [P, KF, DM], F32R)
        gel = sb("gel", [P, 2, HALF])
        hid = sb("hid", [P, 2, HALF])
        hid_hi = sb("hid_hi", [P, 2, HALF], F32R)
        hid_lo = sb("hid_lo", [P, 2, HALF], F32R)
        yT = sb("yT", [P, KD, HALF])
        rows_out = sb("rows_out", [P, 4, DM])

        s_const = sem("const_set")
        s_identz = sem("ident_zeroed")
        s_fill = sem("buffers_filled")
        FILLS = 2 * 4 + 2 * 2 * 2
        s_pickz = sem("pick_zeroed")
        s_const_v = sem("const_set_dve")
        s_vec = sem("vectors_loaded")
        s_vec_turned = sem("vectors_turned")
        s_vecs = sem("vectors_ready")
        s_x = [sem(f"x_loaded{n}") for n in range(NBLK)]
        s_ctx = sem("context_loaded")
        s_xt_ready = sem("x_turned")
        s_xt = sem("x_copied")
        s_ct_ready = sem("context_turned")
        s_ct_hi = sem("context_hi")
        s_ct = sem("context_split")
        s_mean = sem("mean_ready")
        s_cen = sem("centred")
        s_sq = sem("squared")
        s_var = sem("variance_ready")
        s_std = sem("std_ready")
        s_rstd = sem("rstd_ready")
        s_spread = sem("rstd_spread")
        s_nrm = sem("normalised")
        s_aff = sem("affine_done")
        s_bias = sem("bias_added")
        s_hhi = sem("h_hi_ready")
        s_h = sem("h_ready")

        def names(pre):
            return {n: sem(f"{pre}_{n}") for n in (
                "w_loaded", "w_hi", "wq_lo", "w_lo", "wo_loaded", "wo_hi", "wo_lo", "prep_ready", "prep_free0", "prep_free1", "hi_ready",
                "k_twice", "q_lo", "q_again", "x_ready", "x_read", "m_cols", "m_moved0", "m_moved1", "s_ready", "exp_done", "pv_done", "acc_done",
                "sums_ready", "sums_read", "norm_done", "y_ready", "y_added", "o_hi", "o_lo")}

        sems = {SELF: names("self"), CROSS: names("cross")}
        s_w1 = [sem(f"ff_weights_loaded{i}") for i in range(3)]
        s_w1_hi = sem("ff_weights_hi")
        s_w1_lo = sem("ff_weights_split")
        s_gate = sem("gate_ready")
        s_lin = sem("linear_ready")
        s_gel = sem("gelu_done")
        s_hid = sem("hidden_done")
        s_hid_hi = sem("hidden_hi")
        s_hid_lo = sem("hidden_lo")
        s_y = sem("y_step")
        s_yT = sem("y_added")
        s_turn = sem("y_turned")
        s_rows = sem("rows_copied")
        s_out = sem("out_stored")

        W = {SELF: (io["sa_wq"], io["sa_wk"], io["sa_wv"], io["sa_wo"]),
             CROSS: (io["ca_wq"], io["ca_wk"], io["ca_wv"], io["ca_wo"])}
        SRC = {SELF: (h_hi, h_lo), CROSS: (c_hi, c_lo)}
        SC, PV, PREP, FOLD = 0, 2, 6, 7

        def prep_use(plan, kind, a, J, b):
            use = plan.at[kind] + a
            which = (plan.nprep * b + use) % plan.prep_banks
            g = plan.nprep * J + use
            return g, PREP - which, sems[plan][f"prep_free{which}"], g if plan.prep_banks == 1 else g // 2

        def cols(start, n):
            return bass.ds(start, n)

        block = ctx.enter_context(nc.Block())

        @block.sync
        def _(sp):
            def load_x(n):
                t = HALF // P
                sp.dma_start(x_in[:, n * t:(n + 1) * t, :],
                             io["x"].rearrange("b (t p) d -> p (b t) d", p=P)[:, n * t:(n + 1) * t, :]).then_inc(s_x[n], 16)

            load_x(0)
            load_x(1)
            for i, (g, b, nb) in enumerate((("ln1_g", "ln1_b", "sa_bo"), ("ln2_g", "ln2_b", "ca_bo"), ("ln3_g", "ln3_b", "ff_b2"))):
                for v, name in enumerate((g, b, nb)):
                    r = i * NORM_V + v * KD
                    sp.dma_start(vec_rows[r:r + KD, :], io[name].rearrange("(k p) -> k p", p=P)).then_inc(s_vec, 16)
            sp.dma_start(vec_rows[3 * NORM_V:, :], io["ff_b1"].rearrange("(k p) -> k p", p=P)).then_inc(s_vec, 16)
            load_x(2)
            load_x(3)
            sp.dma_start(c_in[:], io["ctx"].rearrange("b (t p) d -> p (b t) d", p=CROSS.ks)).then_inc(s_ctx, 16)

            def attention(plan, h_count):
                S = sems[plan]
                kk, kl = keys_hh[plan], keys_lm[plan]
                wq, wk, wv, wo = W[plan]

                def load_w(J):
                    p0 = fixed(sp, (J % PAIRS) * P)
                    after(sp, S["w_lo"], J)
                    for i, w in enumerate((wq, wk, wv)):
                        n, kin = (P, KD) if i == 0 else (plan.pin, plan.kin)
                        sp.dma_start(w_raw[0:n, i, 0:kin, :],
                                     w.rearrange("(k p) c -> p k c", p=n)[:, :, cols(p0, P)]).then_inc(S["w_loaded"], 16)

                def load_wo(J):
                    p0 = fixed(sp, (J % PAIRS) * P)
                    after(sp, S["wo_lo"], J)
                    sp.dma_start(wo_raw[:], wo[cols(p0, P), :]).then_inc(S["wo_loaded"], 16)

                def emit(steps, par):
                    for kind, J, a, dp in steps:
                        b = par ^ dp
                        if kind in plan.at:
                            g, prep, free, reads = prep_use(plan, kind, a, J, b)
                        if kind == "W":
                            load_w(J)
                            if plan is CROSS and isinstance(J, int) and J == 0:
                                sp.wait_ge(sems[SELF]["y_added"], 4 * NPAIR)
                                for k in range(KD):
                                    sp.dma_start(w1_raw[:, k, :],
                                                 io["ff_w1"].rearrange("(k p) c -> p k c", p=P)[:, k, :]).then_inc(s_w1[k], 16)
                                sp.dma_start(w2_raw[:], io["ff_w2"].rearrange("(k p) c -> p k c", p=P)).then_inc(s_w1[2], 16)
                        elif kind == "L":
                            load_wo(J)
                        elif kind == "M":
                            sp.wait_ge(free, reads + 1)
                            for h in range(2):
                                row = DH if h == 0 else 0
                                sp.dma_start(qm[b][row:row + 1, h, a * HALF:(a + 1) * HALF].rearrange("o (t c) -> o t c", t=4).bitcast(F32),
                                             m_rows[a][4 * h:4 * h + 4, :].bitcast(F32)).then_inc(S[f"m_moved{a}"], 16)

                if plan is CROSS:
                    sp.wait_ge(sems[SELF]["w_lo"], NPAIR)
                bodies("sp", sp, plan, emit)

            attention(SELF, NBLK)
            attention(CROSS, 2 * NBLK)
            out_v = out.rearrange("b (n t p) d -> p (b n) t d", p=P, t=4)
            with sp.Fori(0, NBLK) as n:
                for r in range(2):
                    sp.wait_ge(s_rows, 2 * n + r + 1)
                    sp.dma_start(out_v[:, cols(n, 1), 2 * r:2 * r + 2, :].rearrange("p o t d -> p (o t) d"),
                                 rows_out[:, 2 * r:2 * r + 2, :]).then_inc(s_out, 16)
            sp.wait_ge(s_out, 32 * NBLK)

        @block.tensor
        def _(pe):
            def bank(n, width=HALF):
                return psum[:, n, 0:width]

            def turn_in(n):
                pe.wait_ge(s_x[n], 16)
                for k in range(KD):
                    i = KD * n + k
                    after(pe, s_xt, i - 3)
                    for t in range(4):
                        mm = pe.transpose(psum[:, 4 + i % 4, t * P:(t + 1) * P], x_in[:, 4 * n + t, k * P:(k + 1) * P], ident[:])
                    mm.then_inc(s_xt_ready, 1)

            def turn_vectors():
                pe.wait_ge(s_vec, 16 * 10)
                pe.transpose(psum[:, 3, 0:3 * NORM_V + FF_V], vec_rows[:], ident[0:3 * NORM_V + FF_V, 0:3 * NORM_V + FF_V]).then_inc(s_vec_turned, 1)

            def turn_context():
                pe.wait_ge(s_xt, KD * NBLK)
                pe.wait_ge(s_ctx, 16)
                for k in range(KC):
                    for t in range(BATCH * CROSS.kt):
                        mm = pe.transpose(psum[0:PC, 6 + k, t * CROSS.ks:(t + 1) * CROSS.ks],
                                          c_in[:, t, k * PC:(k + 1) * PC], ident[0:CROSS.ks, 0:CROSS.ks])
                    mm.then_inc(s_ct_ready, 1)

            def mean(part, n):
                if part.L == 0:
                    pe.wait_ge(s_xt, KD * (n + 1))
                for k in range(KD):
                    mm = pe.matmul(bank(part.mean_bank[n]), mean_w[:], xT[:, k, n * HALF:(n + 1) * HALF], start=(k == 0), stop=(k == KD - 1))
                mm.then_inc(s_mean, 1)

            def variances(part):
                for n in part.blocks:
                    pe.wait_ge(s_sq, NBLK * part.L + n + 1)
                    for k in range(KD):
                        mm = pe.matmul(psum[VROWS * (n % 2):VROWS * (n % 2 + 1), part.var_bank, :], mean_w[:, 0:VROWS],
                                       sq[n][:, k, :], start=(k == 0), stop=(k == KD - 1))
                mm.then_inc(s_var, 1)

            def spread(part):
                pe.wait_ge(s_rstd, part.number + 1)
                for n in part.blocks:
                    pe.matmul(bank(part.mean_bank[n]), pick[:, n % 2, :], part.rstd[:], start=True, stop=True).then_inc(s_spread, 1)

            def normalise(L):
                if L == 0:
                    first, second = parts(0)
                    pe.wait_ge(s_const, 1)
                    pe.wait_ge(s_const_v, 1)
                    turn_in(0)
                    turn_in(1)
                    mean(first, 0)
                    turn_vectors()
                    turn_in(2)
                    mean(first, 1)
                    turn_in(3)
                    mean(second, 2)
                    pe.wait_ge(s_vecs, 1)
                    mean(second, 3)
                    turn_context()
                else:
                    S = sems[SELF if L == 1 else CROSS]
                    pe.wait_ge(S["y_added"], 4 * NPAIR)
                    second = parts(L)[1]
                    for n in second.blocks:
                        mean(second, n)
                for part in parts(L):
                    variances(part)
                for part in parts(L):
                    spread(part)

            def attention(plan, h_count):
                S = sems[plan]
                kk, kl = keys_hh[plan], keys_lm[plan]
                src_hi, src_lo = SRC[plan]

                def project(which, src, kin, pin, c0, n, prep):
                    hi, lo = src
                    for k in range(kin):
                        a_hi, a_lo = w_hi[0:pin, which, k, :], w_lo[0:pin, which, k, :]
                        x_hi, x_lo = hi[0:pin, k, cols(c0, n)], lo[0:pin, k, cols(c0, n)]
                        for m, (w, x) in enumerate(((a_hi, x_hi), (a_hi, x_lo), (a_lo, x_hi))):
                            mm = pe.matmul(bank(prep, n), w, x, start=(k == 0 and m == 0), stop=(k == kin - 1 and m == 2))
                    return mm

                def emit(steps, par):
                    for kind, J, a, dp in steps:
                        b = par ^ dp
                        if kind in plan.at:
                            g, prep, free, reads = prep_use(plan, kind, a, J, b)
                        if kind in "KQV":
                            if kind == "K" and a == 0 and isinstance(J, int) and J == 1:
                                pe.wait_ge(s_h, h_count)
                            if kind == "K" and a == 0:
                                pe.wait_ge(S["w_lo"], J + 1)
                            after(pe, free, reads)
                            if kind == "Q":
                                mm = project(0, (h_hi, h_lo), KD, P, (J // PAIRS) * SEQ + a * HALF, HALF, prep)
                            else:
                                c0, n = plan.kcols[a]
                                mm = project(1 if kind == "K" else 2, (src_hi, src_lo), plan.kin, plan.pin,
                                             (J // PAIRS) * plan.keys + c0, n, prep)
                            mm.then_inc(S["prep_ready"], 1)
                        elif kind == "T":
                            _, _, projected, value_reads = prep_use(plan, "V", a, J, b)
                            pe.wait_ge(projected, value_reads + 1)
                            pe.wait_ge(free, reads)
                            n = plan.kt // plan.khalf
                            for t in range(n):
                                mm = pe.transpose(psum[0:plan.ks, prep, t * P:(t + 1) * P],
                                                  valT[:, a, t * plan.ks:(t + 1) * plan.ks], ident[:])
                            mm.then_inc(S["prep_ready"], 1)
                        elif kind == "X":
                            n = plan.tiles * J + a
                            if a == 0:
                                pe.wait_ge(S["k_twice"], plan.khalf * (J + 1))
                            if a in (0, plan.tiles // 2):
                                if plan is CROSS:
                                    pe.wait_ge(S["q_lo"], 4 * J + 2 + 2 * (a // (plan.tiles // 2)))
                                else:
                                    _, _, split, reads = prep_use(plan, "Q", a // (plan.tiles // 2), J, b)
                                    pe.wait_ge(split, reads + 1)
                            after(pe, S["x_read"], n - plan.mx_banks + 1)
                            if plan.khalf == 2:
                                half, h, t, kh = a // 16, a // 2 % 2, a // 4 % 4, a % 2
                                q0 = half * HALF + t * P
                                mm = pe.matmul(bank(PV + plan.pv_banks + a % plan.mx_banks), qq[b][:, h, q0:q0 + P], kk[b][:, h, kh * HALF:(kh + 1) * HALF],
                                               start=True, stop=True)
                            else:
                                for h in range(2):
                                    mm = pe.matmul(psum[:, PV + plan.pv_banks + a % plan.mx_banks, h * plan.keys:(h + 1) * plan.keys],
                                                   qq[b][:, h, a * P:(a + 1) * P], kk[b][:, h, 0:plan.keys], start=True, stop=True)
                            mm.then_inc(S["x_ready"], 1)
                        elif kind == "M":
                            pe.wait_ge(S["m_cols"], 2 * J + a + 1)
                            pe.wait_ge(free, reads)
                            pe.transpose(psum[:, prep, 0:P], m_cols[a][:], ident[:]).then_inc(S["prep_ready"], 1)
                        elif kind == "S":
                            u, h = a
                            half, kt = u // plan.kt, u % plan.kt
                            if kt == 0 and h == 0:
                                if half == 0:
                                    _, _, split, reads = prep_use(plan, "K", plan.khalf - 1, J, b)
                                    pe.wait_ge(split, reads + 1)
                                pe.wait_ge(S["q_again"], 2 * J + half + 1)
                                pe.wait_ge(S[f"m_moved{half}"], 32 * (J + 1))
                            ks = slice(kt * plan.ks, (kt + 1) * plan.ks)
                            qs = slice(half * HALF, (half + 1) * HALF)
                            after(pe, S["exp_done"], 2 * plan.units * J + 2 * u + h - 1)
                            pe.matmul(psum[0:plan.ks, SC + h, :], kk[b][:, h, ks], qq[b][:, h, qs], start=True, stop=False)
                            pe.matmul(psum[0:plan.ks, SC + h, :], kl[b][:, h, ks], qm[b][:, h, qs],
                                      start=False, stop=True).then_inc(S["s_ready"], 1)
                        elif kind == "P":
                            half, kt = a // plan.kt, a % plan.kt
                            if kt == 0:
                                after(pe, S["norm_done"], 2 * J + half + 1 - plan.pv_banks)
                                if half == 0:
                                    _, _, turned, reads = prep_use(plan, "T", plan.khalf - 1, J, b)
                                    pe.wait_ge(turned, reads + 1)
                            pe.wait_ge(S["exp_done"], 2 * plan.units * J + 2 * a + 2)
                            for h in range(2):
                                d = slice(h * DH, (h + 1) * DH)
                                mm = pe.matmul(psum[d, PV + half % plan.pv_banks, :], val[b][0:plan.ks, kt, d], probs[a % 4][0:plan.ks, h, :],
                                               start=(kt == 0), stop=(kt == plan.kt - 1))
                            mm.then_inc(S["pv_done"], 1)
                        elif kind == "D":
                            pe.wait_ge(S["acc_done"], (plan.kt - 1) * (2 * J + a + 1))
                            if a:
                                pe.wait_ge(S["sums_read"], 2 * J + 1)
                            after(pe, S["y_added"], 4 * J - 2 + 2 * a)
                            for h in range(2):
                                mm = pe.matmul(psum[h * DH:(h + 1) * DH, FOLD, :], ones[0:plan.ks, :], acc[a][0:plan.ks, h, :],
                                               start=True, stop=True)
                            mm.then_inc(S["sums_ready"], 1)
                        elif kind == "Y":
                            half, m = a
                            if m == 0:
                                pe.wait_ge(S["o_lo"], 2 * J + half + 1)
                                pe.wait_ge(S["wo_lo"], J + 1)
                            if m or (isinstance(J, int) and J == NPAIR - 1 and half == 1):
                                pe.wait_ge(S["y_added"], 4 * J + 2 * half + m)
                            else:
                                pe.wait_ge(S["sums_read"], 2 * J + 2 + half)
                            mc = slice(m * P, (m + 1) * P)
                            pe.matmul(bank(FOLD), wo_hi[b][:, mc], o_hi[:], start=True, stop=False)
                            pe.matmul(bank(FOLD), wo_hi[b][:, mc], o_lo[:], start=False, stop=False)
                            pe.matmul(bank(FOLD), wo_lo[b][:, mc], o_hi[:], start=False, stop=True).then_inc(S["y_ready"], 1)

                pe.wait_ge(s_h, h_count - NBLK // 2)
                pe.wait_ge(s_fill, FILLS)
                if plan is CROSS:
                    pe.wait_ge(s_ct, KC)

                def ending():
                    first = parts(1 if plan is SELF else 2)[0]
                    pe.wait_ge(S["y_added"], 4 * PAIRS)
                    for n in first.blocks:
                        mean(first, n)

                bodies("pe", pe, plan, emit, ending=ending)

            def feed_forward():
                def turn(n):
                    pe.wait_ge(s_yT, n + 1)
                    after(pe, s_rows, 2 * n)
                    for t in range(4):
                        for m in range(KD):
                            mm = pe.transpose(psum[:, 6 + t // 2, (t % 2) * DM + m * P:(t % 2) * DM + (m + 1) * P],
                                              yT[:, m, t * P:(t + 1) * P], ident[:])
                        if t % 2:
                            mm.then_inc(s_turn, 1)

                def down(n, f):
                    q = KF * n + f
                    if f == 0:
                        after(pe, s_yT, n)
                    if isinstance(n, int) and n == 0 and f == 0:
                        pe.wait_ge(s_w1_lo, KD + 1)
                    pe.wait_ge(s_hid_lo, q + 1)
                    for m in range(KD):
                        mc = slice(m * P, (m + 1) * P)
                        for i, (w, x) in enumerate(((w2_hi, hid_hi), (w2_hi, hid_lo), (w2_lo, hid_hi))):
                            mm = pe.matmul(bank(4 + m), w[:, f, mc], x[:, f % 2, :], start=(f == 0 and i == 0),
                                           stop=(f == KF - 1 and i == 2))
                    mm.then_inc(s_y, 1)

                def one(n, tail):
                    for f in range(KF):
                        q = KF * n + f
                        for c, bk, ready, read in ((DFF + f * P, 2 + f % 2, s_gate, s_gel), (f * P, f % 2, s_lin, s_hid)):
                            after(pe, read, q - 1)
                            for k in range(KD):
                                for i, (w, x) in enumerate(((w1_hi, h_hi), (w1_hi, h_lo), (w1_lo, h_hi))):
                                    mm = pe.matmul(bank(bk), w[:, k, c:c + P], x[:, k, cols(n * HALF, HALF)],
                                                   start=(k == 0 and i == 0), stop=(k == KD - 1 and i == 2))
                            mm.then_inc(ready, 1)
                        if f:
                            down(n, f - 1)
                        if f == 2 and tail:
                            turn(n - 1)
                    down(n, KF - 1)

                pe.wait_ge(s_w1_lo, KD)
                pe.wait_ge(s_h, 3 * NBLK - NBLK // 2)
                one(0, False)
                pe.wait_ge(s_h, 3 * NBLK)
                with pe.Fori(1, NBLK) as n:
                    one(n, True)
                turn(NBLK - 1)

            normalise(0)
            attention(SELF, NBLK)
            normalise(1)
            attention(CROSS, 2 * NBLK)
            normalise(2)
            feed_forward()

        @block.vector
        def _(dve):
            dve.memset(mean_w[:], 1.0 / DM)
            dve.memset(eps[:], EPS)
            dve.memset(pick[:], 0.0).then_inc(s_pickz, 1)
            dve.wait_ge(s_pickz, 1)
            for i in range(2):
                dve.memset(pick[VROWS * i:VROWS * i + 1, i, :], 1.0)
            dve.memset(ones[:], 1.0).then_inc(s_const_v, 1)
            def copy_in(n):
                for k in range(KD):
                    i = KD * n + k
                    dve.wait_ge(s_xt_ready, i + 1)
                    dve.tensor_copy(xT[:, k, n * HALF:(n + 1) * HALF], psum[:, 4 + i % 4, :]).then_inc(s_xt, 1)

            def centre(part, n):
                dve.wait_ge(s_mean, NBLK * part.L + n + 1)
                dve.tensor_tensor(cen[n][:], xT[:, :, n * HALF:(n + 1) * HALF],
                                  psum[:, part.mean_bank[n], :].unsqueeze(1).to_broadcast([P, KD, HALF]), ALU.subtract).then_inc(s_cen, 1)

            def invert(part):
                dve.wait_ge(s_std, part.number + 1)
                dve.reciprocal(part.rstd[:], part.rstd[:]).then_inc(s_rstd, 1)

            def scale(part, n):
                dve.wait_ge(s_spread, NBLK * part.L + n + 1)
                dve.tensor_tensor(cen[n][:], cen[n][:],
                                  psum[:, part.mean_bank[n], :].unsqueeze(1).to_broadcast([P, KD, HALF]), ALU.mult).then_inc(s_nrm, 1)

            def low(part, n):
                dve.wait_ge(s_hhi, NBLK * part.L + n + 1)
                dve.tensor_tensor(h_lo[:, :, n * HALF:(n + 1) * HALF], sq[n][:], h_hi[:, :, n * HALF:(n + 1) * HALF],
                                  ALU.subtract).then_inc(s_h, 1)

            def normalise(L):
                if L == 0:
                    first, second = parts(0)
                    copy_in(0)
                    copy_in(1)
                    dve.wait_ge(s_vec_turned, 1)
                    dve.tensor_copy(vecs[:], psum[:, 3, 0:3 * NORM_V + FF_V]).then_inc(s_vecs, 1)
                    centre(first, 0)
                    copy_in(2)
                    centre(first, 1)
                    copy_in(3)
                    centre(second, 2)
                    centre(second, 3)
                    for k in range(KC):
                        dve.wait_ge(s_ct_hi, k + 1)
                        dve.tensor_tensor(c_lo[:, k, :], psum[0:PC, 6 + k, 0:BATCH * TC], c_hi[:, k, :], ALU.subtract).then_inc(s_ct, 1)
                else:
                    second = parts(L)[1]
                    for n in second.blocks:
                        centre(second, n)
                for part in parts(L):
                    invert(part)
                blocks = [(part, n) for part in parts(L) for n in part.blocks]
                for i in range(NBLK + 2):
                    if i < NBLK:
                        scale(*blocks[i])
                    if i >= 2:
                        low(*blocks[i - 2])

            def attention(plan, h_count):
                S = sems[plan]
                kk, kl = keys_hh[plan], keys_lm[plan]

                def emit(steps, par):
                    for kind, J, a, dp in steps:
                        b = par ^ dp
                        if kind in plan.at:
                            g, prep, free, reads = prep_use(plan, kind, a, J, b)
                        if kind == "K" or (kind == "Q" and plan is SELF):
                            c0, n = plan.kcols[a] if kind == "K" else (a * HALF, HALF)
                            hi, lo = (kk[b], kl[b]) if kind == "K" else (qq[b], qq[b])
                            dve.wait_ge(S["hi_ready"], plan.nsplit * J + plan.at[kind] + a + 1)
                            for h in range(2):
                                own = slice(h * DH, (h + 1) * DH)
                                to = own if kind == "K" else slice((1 - h) * DH, (2 - h) * DH)
                                op = dve.tensor_tensor(lo[to, h, c0:c0 + n], psum[own, prep, 0:n], hi[own, h, c0:c0 + n], ALU.subtract)
                            op.then_inc(free, 1)
                        elif kind == "X":
                            dve.wait_ge(S["x_ready"], plan.tiles * J + a + 1)
                            if plan.khalf == 2:
                                half, h, t, kh = a // 16, a // 2 % 2, a // 4 % 4, a % 2
                                dve.tensor_reduce(m_part[:, half, h, t, kh:kh + 1], psum[:, PV + plan.pv_banks + a % plan.mx_banks, :], AX.X,
                                                  ALU.max).then_inc(S["x_read"], 1)
                            else:
                                dve.tensor_reduce(m_part[:, a // 4, :, a % 4, 0],
                                                  psum[:, PV + plan.pv_banks + a % plan.mx_banks, 0:2 * plan.keys].rearrange("p (h k) -> p h k", h=2),
                                                  AX.X, ALU.max).then_inc(S["x_read"], 1)
                        elif kind == "C":
                            dve.wait_ge(S["x_read"], plan.tiles * J + plan.tiles // 2 * (a + 1))
                            dve.tensor_reduce(m_cols[a][:, 0:8], m_part[:, a, :, :, 0:plan.khalf].rearrange("p h t k -> p (h t) k"),
                                              AX.X, ALU.max).then_inc(S["m_cols"], 1)
                        elif kind == "M":
                            after(dve, S[f"m_moved{a}"], 32 * J)
                            dve.wait_ge(S["prep_ready"], g + 1)
                            dve.tensor_copy(m_rows[a][:], psum[0:8, prep, 0:P]).then_inc(free, 1)
                        elif kind == "D":
                            dve.wait_ge(S["sums_ready"], 2 * J + a + 1)
                            after(dve, S["norm_done"], 2 * J + a)
                            dve.reciprocal(recip[:], psum[:, FOLD, :]).then_inc(S["sums_read"], 1)
                        elif kind == "R":
                            dve.wait_ge(S["sums_read"], 2 * J + a + 1)
                            dve.wait_ge(S["pv_done"], plan.units * J + plan.kt * (a + 1))
                            after(dve, S["o_lo"], 2 * J + a)
                            dve.tensor_tensor(oT[:], psum[:, PV + a % plan.pv_banks, :], recip[:], ALU.mult).then_inc(S["norm_done"], 1)
                        elif kind == "Y":
                            half, m = a
                            dve.wait_ge(S["y_ready"], 4 * J + 2 * half + m + 1)
                            x = xT[:, m, cols((J // PAIRS) * SEQ + half * HALF, HALF)]
                            dve.tensor_tensor(x, x, psum[:, FOLD, :], ALU.add).then_inc(S["y_added"], 1)

                dve.wait_ge(s_h, h_count)
                dve.wait_ge(s_bias, h_count)

                def ending():
                    first = parts(1 if plan is SELF else 2)[0]
                    for n in first.blocks:
                        centre(first, n)

                bodies("dve", dve, plan, emit, ending=ending)

            def feed_forward():
                dve.wait_ge(s_bias, 3 * NBLK)

                def lo(n, f):
                    q = KF * n + f
                    dve.wait_ge(s_hid_hi, q + 1)
                    dve.tensor_tensor(hid_lo[:, f % 2, :], hid[:, f % 2, :], hid_hi[:, f % 2, :], ALU.subtract).then_inc(s_hid_lo, 1)

                def one(n):
                    for f in range(KF):
                        q = KF * n + f
                        dve.wait_ge(s_gel, q + 1)
                        dve.wait_ge(s_lin, q + 1)
                        if f >= 2 or not isinstance(n, int):
                            after(dve, s_hid_lo, q - 1)
                        dve.scalar_tensor_tensor(hid[:, f % 2, :], psum[:, f % 2, :], ff_b1(f), gel[:, f % 2, :],
                                                 ALU.add, ALU.mult).then_inc(s_hid, 1)
                        lo(n, f)
                    dve.wait_ge(s_y, KF * (n + 1))
                    after(dve, s_turn, 2 * n)
                    dve.tensor_tensor(yT[:], psum[:, 4:6, :], xT[:, :, cols(n * HALF, HALF)], ALU.add).then_inc(s_yT, 1)

                one(0)
                with dve.Fori(1, NBLK) as n:
                    one(n)

            normalise(0)
            attention(SELF, NBLK)
            normalise(1)
            attention(CROSS, 2 * NBLK)
            normalise(2)
            feed_forward()

        @block.scalar
        def _(act):
            def square(part, n):
                act.wait_ge(s_cen, NBLK * part.L + n + 1)
                act.activation(sq[n][:], cen[n][:], ACT.Square).then_inc(s_sq, 1)

            def root(part):
                act.wait_ge(s_var, part.number + 1)
                act.activation(part.rstd[:], psum[:, part.var_bank, :], ACT.Sqrt, bias=eps[:]).then_inc(s_std, 1)

            def affine(part, n):
                L = part.L
                act.wait_ge(s_nrm, NBLK * L + n + 1)
                for k in range(KD):
                    op = act.activation(sq[n][:, k, :], cen[n][:, k, :], ACT.Identity, scale=ln_g(L, k), bias=ln_b(L, k))
                op.then_inc(s_aff, 1)
                act.wait_ge(s_aff, NBLK * L + n + 1)
                act.activation(h_hi[:, :, n * HALF:(n + 1) * HALF], sq[n][:], ACT.Copy).then_inc(s_hhi, 1)

            def normalise(L):
                if L == 0:
                    act.wait_ge(s_const_v, 1)
                for part in parts(L):
                    for n in part.blocks:
                        square(part, n)
                if L == 0:
                    for k in range(KC):
                        act.wait_ge(s_ct_ready, k + 1)
                        act.activation(c_hi[:, k, :], psum[0:PC, 6 + k, 0:BATCH * TC], ACT.Copy).then_inc(s_ct_hi, 1)
                for part in parts(L):
                    root(part)
                if L == 0:
                    act.wait_ge(s_vecs, 1)
                for part in parts(L):
                    for n in part.blocks:
                        affine(part, n)

            def attention(plan, h_count):
                S = sems[plan]
                kk, kl = keys_hh[plan], keys_lm[plan]

                def split_w(J):
                    act.wait_ge(S["w_loaded"], 48 * (J + 1))
                    after(act, S["prep_ready"], plan.nprep * (J - 1) + plan.at["T"])
                    if plan is SELF:
                        act.activation(w_hi[:], w_raw[:], ACT.Copy).then_inc(S["w_hi"], 1)
                    else:
                        act.activation(w_hi[:, 0, :, :], w_raw[:, 0, :, :], ACT.Copy).then_inc(S["w_hi"], 1)
                        act.activation(w_hi[0:PC, 1:3, :, :], w_raw[0:PC, 1:3, :, :], ACT.Copy).then_inc(S["w_hi"], 1)

                def emit(steps, par):
                    for kind, J, a, dp in steps:
                        b = par ^ dp
                        if kind in plan.at:
                            g, prep, free, reads = prep_use(plan, kind, a, J, b)
                        if kind == "W":
                            split_w(J)
                        elif kind == "O":
                            act.wait_ge(S["wo_loaded"], 16 * (J + 1))
                            after(act, S["y_ready"], 4 * (J - 1))
                            act.activation(wo_hi[b][:], wo_raw[:], ACT.Copy).then_inc(S["wo_hi"], 1)
                        elif kind == "K":
                            c0, n = plan.kcols[a]
                            act.wait_ge(S["prep_ready"], g + 1)
                            if a == 0:
                                after(act, S["s_ready"], 2 * plan.units * (J - 1))
                            for h in range(2):
                                own = slice(h * DH, (h + 1) * DH)
                                op = act.activation(kk[b][own, h, c0:c0 + n], psum[own, prep, 0:n], ACT.Copy)
                            op.then_inc(S["hi_ready"], 1)
                            act.wait_ge(S["hi_ready"], plan.nsplit * J + a + 1)
                            for h in range(2):
                                own, other = slice(h * DH, (h + 1) * DH), slice((1 - h) * DH, (2 - h) * DH)
                                op = act.activation(kk[b][other, h, c0:c0 + n], kk[b][own, h, c0:c0 + n], ACT.Copy)
                            op.then_inc(S["k_twice"], 1)
                        elif kind == "Q":
                            act.wait_ge(S["prep_ready"], g + 1)
                            for h in range(2):
                                own = slice(h * DH, (h + 1) * DH)
                                op = act.activation(qq[b][own, h, a * HALF:(a + 1) * HALF], psum[own, prep, :], ACT.Copy)
                            op.then_inc(S["hi_ready"], 1)
                            if plan is CROSS:
                                after(act, S["q_lo"], 4 * J + 2 * a - 2)
                                act.activation(q_full[:, a, :], psum[:, prep, :], ACT.Copy).then_inc(free, 1)
                        elif kind == "B":
                            act.wait_ge(S["hi_ready"], plan.nsplit * J + plan.khalf + a + 1)
                            for h in range(2):
                                own, half = slice(h * DH, (h + 1) * DH), slice(a * HALF, (a + 1) * HALF)
                                op = act.activation(qm[b][own, h, half], qq[b][own, h, half], ACT.Copy)
                            op.then_inc(S["q_again"], 1)
                        elif kind == "V":
                            act.wait_ge(S["prep_ready"], g + 1)
                            n = plan.kcols[a][1]
                            act.activation(valT[:, a, 0:n], psum[:, prep, 0:n], ACT.Copy).then_inc(free, 1)
                        elif kind == "T":
                            act.wait_ge(S["prep_ready"], g + 1)
                            after(act, S["pv_done"], plan.units * (J - 1))
                            n = plan.kt // plan.khalf
                            act.activation(val[b][0:plan.ks, a * n:(a + 1) * n, :],
                                           psum[0:plan.ks, prep, 0:n * P].rearrange("p (t d) -> p t d", t=n),
                                           ACT.Copy).then_inc(free, 1)
                        elif kind == "S":
                            u, h = a
                            if h == 0:
                                after(act, S["pv_done"], plan.units * J + u - 3)
                                pair, back = (J, u - 4) if u >= 4 else (J - 1, u - 4 + plan.units)
                                after(act, S["acc_done"], 2 * (plan.kt - 1) * pair + plan.added(back))
                            act.wait_ge(S["s_ready"], 2 * plan.units * J + 2 * u + h + 1)
                            act.activation(probs[u % 4][0:plan.ks, h, :], psum[0:plan.ks, SC + h, :], ACT.Exp,
                                           scale=SCALE).then_inc(S["exp_done"], 1)
                        elif kind == "N":
                            act.wait_ge(S["norm_done"], 2 * J + a + 1)
                            after(act, S["y_ready"], 4 * J + 2 * a)
                            act.activation(o_hi[:], oT[:], ACT.Copy).then_inc(S["o_hi"], 1)

                if plan is CROSS:
                    act.wait_ge(sems[SELF]["prep_ready"], SELF.nprep * NPAIR)
                    act.wait_ge(sems[SELF]["w_lo"], NPAIR)
                bodies("act", act, plan, emit, (lambda: normalise(1)) if plan is CROSS else None)

            def feed_forward():
                act.wait_ge(s_vecs, 1)

                def hi(n, f):
                    q = KF * n + f
                    act.wait_ge(s_hid, q + 1)
                    after(act, s_y, q - 1)
                    act.activation(hid_hi[:, f % 2, :], hid[:, f % 2, :], ACT.Copy).then_inc(s_hid_hi, 1)

                def store(n):
                    for r in range(2):
                        act.wait_ge(s_turn, 2 * n + r + 1)
                        after(act, s_out, 32 * n)
                        act.activation(rows_out[:, 2 * r:2 * r + 2, :],
                                       psum[:, 6 + r, :].rearrange("p (t d) -> p t d", t=2), ACT.Copy).then_inc(s_rows, 1)

                def one(n, tail):
                    for f in range(KF):
                        q = KF * n + f
                        if f:
                            hi(n, f - 1)
                        act.wait_ge(s_gate, q + 1)
                        after(act, s_hid, q - 1)
                        act.activation(gel[:, f % 2, :], psum[:, 2 + f % 2, :], ACT.Gelu,
                                       bias=ff_b1(KF + f)).then_inc(s_gel, 1)
                        if f == 3 and tail:
                            store(n - 1)
                    hi(n, KF - 1)

                one(0, False)
                with act.Fori(1, NBLK) as n:
                    one(n, True)
                store(NBLK - 1)

            normalise(0)
            attention(SELF, NBLK)
            attention(CROSS, 2 * NBLK)
            act.wait_ge(sems[CROSS]["y_added"], 4 * NPAIR)
            act.wait_ge(sems[CROSS]["w_lo"], NPAIR)
            for k in range(KD):
                act.wait_ge(s_w1[k], 16)
                act.activation(w1_hi[:, k, :], w1_raw[:, k, :], ACT.Copy).then_inc(s_w1_hi, 1)
            act.wait_ge(s_w1[2], 16)
            act.activation(w2_hi[:], w2_raw[:], ACT.Copy).then_inc(s_w1_hi, 1)
            normalise(2)
            feed_forward()

        @block.gpsimd
        def _(pool):
            pool.memset(ident[:], 0.0).then_inc(s_identz, 1)
            pool.wait_ge(s_identz, 1)
            pool.affine_select(out=ident[:], in_=ident[:], compare_op=ALU.not_equal, fill=1.0, base=0,
                               pattern=[[-1, P]], channel_multiplier=1).then_inc(s_const, 1)
            filled = 0
            for b in range(2):
                for buffer in (m_cols[b], qm[b], keys_lm[SELF][b], keys_lm[CROSS][b]):
                    filled += 1
                    pool.memset(buffer[:].bitcast(F32), 0.0).then_inc(s_fill, 1)
            for b in range(2):
                for plan in (SELF, CROSS):
                    for h, row in ((0, DH), (1, 0)):
                        pool.wait_ge(s_fill, filled)
                        filled += 1
                        pool.memset(keys_lm[plan][b][row:row + 1, h, :].bitcast(F32), -1.0).then_inc(s_fill, 1)
            pool.wait_ge(s_fill, FILLS)

            def add_bias(L):
                if L == 0:
                    pool.wait_ge(s_vecs, 1)
                for n in range(NBLK):
                    pool.wait_ge(s_cen, NBLK * L + n + 1)
                    for k in range(KD):
                        op = pool.tensor_scalar(xT[:, k, n * HALF:(n + 1) * HALF], xT[:, k, n * HALF:(n + 1) * HALF], out_b(L, k), None, ALU.add)
                    op.then_inc(s_bias, 1)
                pool.wait_ge(s_bias, NBLK * L + n + 1)

            def attention(plan, h_count):
                S = sems[plan]
                kk, kl = keys_hh[plan], keys_lm[plan]

                def split_w(J):
                    if plan is SELF:
                        pool.wait_ge(S["w_hi"], J + 1)
                        pool.tensor_tensor(w_lo[:], w_raw[:], w_hi[:], ALU.subtract).then_inc(S["w_lo"], 1)
                    else:
                        pool.wait_ge(S["w_hi"], 2 * J + 2)
                        pool.tensor_tensor(w_lo[:, 0, :, :], w_raw[:, 0, :, :], w_hi[:, 0, :, :], ALU.subtract).then_inc(S["wq_lo"], 1)
                        pool.wait_ge(S["wq_lo"], J + 1)
                        pool.tensor_tensor(w_lo[0:PC, 1:3, :, :], w_raw[0:PC, 1:3, :, :], w_hi[0:PC, 1:3, :, :],
                                           ALU.subtract).then_inc(S["w_lo"], 1)
                        pool.wait_ge(S["w_lo"], J + 1)

                def emit(steps, par):
                    for kind, J, a, dp in steps:
                        b = par ^ dp
                        if kind in plan.at:
                            g, prep, free, reads = prep_use(plan, kind, a, J, b)
                        if kind == "W":
                            split_w(J)
                        elif kind == "O":
                            pool.wait_ge(S["wo_hi"], J + 1)
                            pool.tensor_tensor(wo_lo[b][:], wo_raw[:], wo_hi[b][:], ALU.subtract).then_inc(S["wo_lo"], 1)
                            if plan is CROSS:
                                pool.wait_ge(S["wo_lo"], J + 1)
                        elif kind == "S":
                            u, h = a
                            half, kt = u // plan.kt, u % plan.kt
                            if kt == 0 or h == 0:
                                continue
                            now, last = probs[u % 4][0:plan.ks], probs[(u - 1) % 4][0:plan.ks]
                            total = acc[half][0:plan.ks]
                            summed = 2 * (plan.kt - 1) * J + plan.added(u)
                            if kt == 1:
                                after(pool, S["sums_ready"], 2 * (J - 1) + half + 1)
                            else:
                                pool.wait_ge(S["acc_done"], summed - 1)
                            pool.wait_ge(S["exp_done"], 2 * plan.units * J + 2 * u + 2)
                            pool.tensor_tensor(total, last if kt == 1 else total, now, ALU.add).then_inc(S["acc_done"], 1)
                            if plan is CROSS:
                                pool.wait_ge(S["acc_done"], summed)
                        elif kind == "Q" and plan is CROSS:
                            pool.wait_ge(S["hi_ready"], plan.nsplit * J + plan.khalf + a + 1)
                            pool.wait_ge(free, reads + 1)
                            for h in range(2):
                                own, other = slice(h * DH, (h + 1) * DH), slice((1 - h) * DH, (2 - h) * DH)
                                half = slice(a * HALF, (a + 1) * HALF)
                                pool.tensor_tensor(qq[b][other, h, half], q_full[own, a, :], qq[b][own, h, half],
                                                   ALU.subtract).then_inc(S["q_lo"], 1)
                                pool.wait_ge(S["q_lo"], 4 * J + 2 * a + h + 1)
                        elif kind == "N":
                            pool.wait_ge(S["o_hi"], 2 * J + a + 1)
                            pool.tensor_tensor(o_lo[:], oT[:], o_hi[:], ALU.subtract).then_inc(S["o_lo"], 1)
                            if plan is CROSS:
                                pool.wait_ge(S["o_lo"], 2 * J + a + 1)

                bodies("pool", pool, plan, emit, (lambda: add_bias(1)) if plan is CROSS else None)

            def split_ff(i, raw, hi, lo):
                pool.wait_ge(s_w1_hi, i + 1)
                pool.tensor_tensor(lo, raw, hi, ALU.subtract).then_inc(s_w1_lo, 1)

            add_bias(0)
            attention(SELF, NBLK)
            attention(CROSS, 2 * NBLK)
            split_ff(0, w1_raw[:, 0, :], w1_hi[:, 0, :], w1_lo[:, 0, :])
            split_ff(1, w1_raw[:, 1, :], w1_hi[:, 1, :], w1_lo[:, 1, :])
            split_ff(2, w2_raw[:], w2_hi[:], w2_lo[:])
            add_bias(2)


_NAMES = {"x": "x", "ctx_768": "ctx"}
_PREFIX = "L0_xattn_"
_INS = ["x", "ctx_768"] + [_PREFIX + n for n in (
    "ln1_g", "ln1_b", "ln2_g", "ln2_b", "ln3_g", "ln3_b", "sa_wq", "sa_wk", "sa_wv", "sa_wo", "sa_bo",
    "ca_wq", "ca_wk", "ca_wv", "ca_wo", "ca_bo", "ff_w1", "ff_b1", "ff_w2", "ff_b2")]


def kernel(**inputs):
    import numpy as _np
    import concourse.bacc as _bacc
    from concourse import mybir as _mybir
    from concourse.bass_utils import run_bass_kernel_spmd as _run

    nc = _bacc.Bacc("TRN2", target_bir_lowering=False, num_devices=1)
    arrays, io = {}, {}
    for name in _INS:
        a = _np.ascontiguousarray(inputs[name])
        arrays[f"in_{name}"] = a
        io[_NAMES.get(name, name.removeprefix(_PREFIX))] = nc.dram_tensor(
            f"in_{name}", a.shape, _mybir.dt.from_np(a.dtype), kind="ExternalInput").ap()
    out = nc.dram_tensor("out", (BATCH, SEQ, DM), _mybir.dt.float32, kind="ExternalOutput").ap()
    block_kernel(nc, io, out)
    r = _run(nc, [arrays], core_ids=[0])
    return r.results[0]["out"]
```
